# Optimizing a Trainium2 kernel written in Bass

```python
import numpy as np
import jax
import jax.numpy as jnp

def _softmax(x, axis=-1):
    return jax.nn.softmax(x, axis=axis)

def _gelu(x):
    return jax.nn.gelu(x, approximate=True)

def _silu(x):
    return jax.nn.silu(x)

def _sigmoid(x):
    return jax.nn.sigmoid(x)

def _layernorm(x, axis=-1, eps=1e-05):
    m = jnp.mean(x, axis=axis, keepdims=True)
    v = jnp.var(x, axis=axis, keepdims=True)
    return (x - m) / jnp.sqrt(v + eps)

def _scatter_add(tgt, idx, src, axis=0):
    return tgt.at[idx].add(src)

def _segment_sum(src, seg, n):
    return jax.ops.segment_sum(src, seg, n)
kernel_name = 'mk_seq_preln_d1_jaxref_r4_53cf51'

def setup_inputs(seed: int=0):
    np.random.seed(seed)
    _w = jnp.asarray

    def _L0_attn_setup():
        import jax, jax.numpy as jnp
        import numpy as np
        import math
        D_MODEL = 256
        N_HEADS = 16
        DECAY_SCALE = 0.25

        def power_law_mask(n, decay_scale):
            i = jnp.arange(n)[:, None]
            j = jnp.arange(n)[None, :]
            delta = (i - j).astype(jnp.float32)
            decay = jnp.where(delta > 0, -decay_scale * jnp.log(jnp.maximum(delta, 1.0)), 0.0)
            return jnp.where(j > i, -jnp.inf, decay)
        key = jax.random.key(seed)
        ks = jax.random.split(key, 9)
        B, N, D = (2, 512, D_MODEL)
        s = 1.0 / math.sqrt(D)
        return {'x': jax.random.normal(ks[0], (B, N, D), dtype=jnp.float32), 'Wq': jax.random.normal(ks[1], (D, D), dtype=jnp.float32) * s, 'bq': jnp.zeros((D,), dtype=jnp.float32), 'Wk': jax.random.normal(ks[2], (D, D), dtype=jnp.float32) * s, 'bk': jnp.zeros((D,), dtype=jnp.float32), 'Wv': jax.random.normal(ks[3], (D, D), dtype=jnp.float32) * s, 'bv': jnp.zeros((D,), dtype=jnp.float32), 'Wo': jax.random.normal(ks[4], (D, D), dtype=jnp.float32) * s, 'bo': jnp.zeros((D,), dtype=jnp.float32)}
    _L0_attn_in = _L0_attn_setup()

    def _L0_ffn_setup():
        import jax, jax.numpy as jnp
        import numpy as np
        DIM = 256
        HIDDEN = 768
        SCALE = 1.0 / 127.0

        def _dequant(w_int, dtype):
            return w_int.astype(dtype) * jnp.asarray(SCALE, dtype)
        key = jax.random.key(seed)
        k_x, k_g, k_u, k_d = jax.random.split(key, 4)
        x = jax.random.normal(k_x, (4, 512, DIM), dtype=jnp.float32)
        w_gate = jax.random.randint(k_g, (HIDDEN, DIM), -127, 128, dtype=jnp.int32)
        w_up = jax.random.randint(k_u, (HIDDEN, DIM), -127, 128, dtype=jnp.int32)
        w_down = jax.random.randint(k_d, (DIM, HIDDEN), -127, 128, dtype=jnp.int32)
        return {'x': x, 'w_gate': w_gate, 'w_up': w_up, 'w_down': w_down}
    _L0_ffn_in = _L0_ffn_setup()
    _d = {'L0_attn_x': _L0_attn_in['x'], 'L0_attn_Wq': _L0_attn_in['Wq'], 'L0_attn_bq': _L0_attn_in['bq'], 'L0_attn_Wk': _L0_attn_in['Wk'], 'L0_attn_bk': _L0_attn_in['bk'], 'L0_attn_Wv': _L0_attn_in['Wv'], 'L0_attn_bv': _L0_attn_in['bv'], 'L0_attn_Wo': _L0_attn_in['Wo'], 'L0_attn_bo': _L0_attn_in['bo'], 'L0_ffn_w_gate': _L0_ffn_in['w_gate'], 'L0_ffn_w_up': _L0_ffn_in['w_up'], 'L0_ffn_w_down': _L0_ffn_in['w_down']}
    _x0 = _d['L0_attn_x']
    _d['L0_attn_x'] = jax.random.normal(jax.random.fold_in(jax.random.key(seed), 1), (4, 2048, 256), dtype=_x0.dtype)
    del _x0
    return _d

def reference(L0_attn_x, L0_attn_Wq, L0_attn_bq, L0_attn_Wk, L0_attn_bk, L0_attn_Wv, L0_attn_bv, L0_attn_Wo, L0_attn_bo, L0_ffn_w_gate, L0_ffn_w_up, L0_ffn_w_down):

    def _L0_attn_ref(x, Wq, bq, Wk, bk, Wv, bv, Wo, bo):
        import jax, jax.numpy as jnp
        import numpy as np
        import math
        D_MODEL = 256
        N_HEADS = 16
        DECAY_SCALE = 0.25

        def power_law_mask(n, decay_scale):
            i = jnp.arange(n)[:, None]
            j = jnp.arange(n)[None, :]
            delta = (i - j).astype(jnp.float32)
            decay = jnp.where(delta > 0, -decay_scale * jnp.log(jnp.maximum(delta, 1.0)), 0.0)
            return jnp.where(j > i, -jnp.inf, decay)
        B, N, D = x.shape
        H = N_HEADS
        dk = D // H

        def proj(W, b):
            return (x @ W + b).reshape(B, N, H, dk).transpose(0, 2, 1, 3)
        Q, K, V = (proj(Wq, bq), proj(Wk, bk), proj(Wv, bv))
        scores = jnp.einsum('bhnd,bhmd->bhnm', Q, K) / jnp.sqrt(jnp.float32(dk))
        scores = scores + power_law_mask(N, DECAY_SCALE)[None, None]
        attn = jax.nn.softmax(scores, axis=-1)
        out = jnp.einsum('bhnm,bhmd->bhnd', attn, V)
        out = out.transpose(0, 2, 1, 3).reshape(B, N, D)
        return out @ Wo + bo

    def _L0_ffn_ref(x, w_gate, w_up, w_down):
        import jax, jax.numpy as jnp
        import numpy as np
        DIM = 256
        HIDDEN = 768
        SCALE = 1.0 / 127.0

        def _dequant(w_int, dtype):
            return w_int.astype(dtype) * jnp.asarray(SCALE, dtype)
        wg = _dequant(w_gate, x.dtype)
        wu = _dequant(w_up, x.dtype)
        wd = _dequant(w_down, x.dtype)
        gate = jnp.einsum('bsd,hd->bsh', x, wg)
        up = jnp.einsum('bsd,hd->bsh', x, wu)
        h = jax.nn.silu(gate) * up
        return jnp.einsum('bsh,dh->bsd', h, wd)
    x = L0_attn_x
    x = x + _L0_attn_ref(_layernorm(x, axis=-1), L0_attn_Wq, L0_attn_bq, L0_attn_Wk, L0_attn_bk, L0_attn_Wv, L0_attn_bv, L0_attn_Wo, L0_attn_bo)
    x = x + _L0_ffn_ref(_layernorm(x, axis=-1), L0_ffn_w_gate, L0_ffn_w_up, L0_ffn_w_down)
    return x

_drawn_inputs = setup_inputs


def setup_inputs(seed=0):
    import zlib

    import numpy as np

    out = dict(_drawn_inputs(seed))
    spreads = {'L0_attn_bq': (0.0, 0.6),
     'L0_attn_bk': (0.0, 0.8),
     'L0_attn_bv': (0.0, 0.1),
     'L0_attn_bo': (0.0, 0.1)}
    factors = {}
    for name, (base, spread) in spreads.items():
        noise = np.random.default_rng([zlib.crc32(name.encode()), seed]).standard_normal(out[name].shape)
        drawn = base * np.exp(spread * noise) if base else spread * noise
        out[name] = jnp.asarray(drawn.astype(out[name].dtype))
    for name, factor in factors.items():
        out[name] = (out[name] * factor).astype(out[name].dtype)
    return out
```

```python
import math
from contextlib import ExitStack

import numpy as np

import concourse.bass as bass
from concourse import mybir

P = 128
B, N, D = 4, 2048, 256
H = 16
DK = D // H
HIDDEN = 768
EPS = 1e-5
DECAY = 0.25
W_SCALE = 1.0 / 127.0
SCORE_SCALE = 1.0 / math.sqrt(DK)
MASKED = -3.0e38

TG = 512
GROUPS = N // TG
DC = D // P
HC = HIDDEN // P
TT = TG // P
HG = 4
NG = B * H // HG
RG = HG * DK
PIECES = 3
Q_SLOTS = (0, 1, 2, 0, 1, 0)
K_SLOTS = (0, 0, 0, 1, 1, 2)
KROWS = len(Q_SLOTS) * DK
SROWS = KROWS + 2
VC = 32
KT = N // P

F32 = mybir.dt.float32
BF16 = mybir.dt.bfloat16
I32 = mybir.dt.int32
ALU = mybir.AluOpType
ACT = mybir.ActivationFunctionType

LAG = 3
PS = 4


def key_tiles(q):
    full, diagonal = list(range(4 * q)), list(range(4 * q, 4 * q + 4))
    return [j for i in range(4) for j in full[i * q:(i + 1) * q] + [diagonal[i]]]


STEPS = [(q, j) for q in range(GROUPS) for j in key_tiles(q)]
NS = len(STEPS)
FIRST = [STEPS.index((q, key_tiles(q)[0])) for q in range(GROUPS)]
LAST = [STEPS.index((q, key_tiles(q)[-1])) for q in range(GROUPS)]


def pool_heads(s):
    q, j = STEPS[s]
    return 0 if j >= 4 * q else HG


POOLED = [s for s in range(NS) if pool_heads(s)]
DVE_DECAYS = sum(HG - pool_heads(s) for s in range(NS))
SB = 3
ITEMS = HG * NS


def first_column(s):
    q, j = STEPS[s]
    return P * max(0, j - 4 * q)


def score_bank(parity, n):
    i = ITEMS * parity + n
    back = SB
    if i < SB:
        last = max(k for k in range(2 * ITEMS) if k % SB == i % SB)
        back = 2 * ITEMS + i - last
    return i % SB, back


def max_chunks(q):
    out = []
    for h in range(HG):
        for r in range(TT):
            width = TG * q + P * (r + 1)
            for part in range((width + 1023) // 1024):
                out.append((h, r, part, 1024 * part, min(1024, width - 1024 * part)))
    return out


def slot_chunks(s, h):
    q = STEPS[s][0]
    steps, i = LAST[q] - FIRST[q] + 1, s - FIRST[q]
    c = max_chunks(q)
    c = c[i * len(c) // steps:(i + 1) * len(c) // steps]
    return c[h * len(c) // HG:(h + 1) * len(c) // HG]


def finalized(s):
    q, i = STEPS[s][0], s - FIRST[STEPS[s][0]]
    return ((q - 1) % GROUPS, i) if i < 4 else None


def opening():
    for q in range(GROUPS):
        for i, chunk in enumerate(max_chunks(q)):
            yield "chunk", q, chunk
            if q and i % 2 and i // 2 < 4:
                yield "stage", q - 1, i // 2


MAX_ITEMS = sum(len(max_chunks(q)) for q in range(GROUPS)) + GROUPS
MAX_FIRST = MAX_ITEMS - 1


def ring_start(s, last):
    n = 0
    for t in range(s):
        if not last:
            n += sum(len(slot_chunks(t, h)) for h in range(HG))
        q, stage = finalized(t) or (0, 0)
        n += stage == 3 and (not last or q == GROUPS - 1)
    return n


def decay_start(s):
    return sum(HG - pool_heads(t) for t in range(s))


def trailing(s):
    return (0, s - LAG) if s >= LAG else (1, s - LAG + NS)


def project(nc, x, wq, bq, wk, bk, wv, bv, ident_in, qs, ks, vs):
    ctx = ExitStack()
    with ctx:
        sb = lambda n, s, d=F32: ctx.enter_context(nc.sbuf_tensor(n, s, d))
        pb = lambda n, s, d=F32: ctx.enter_context(nc.psum_tensor(n, s, d))
        sem = lambda n: ctx.enter_context(nc.semaphore(n))
        w_sb = [sb(f"w_{n}", [P, DC, D]) for n in "qkv"]
        bias = [sb(f"bias_{n}", [P, DC]) for n in "qk"]
        bias_v = sb("bias_v", [P, D])
        ident = sb("ident_a", [P, P])
        xt = [sb(f"x_tok{i}", [P, TT, D]) for i in range(2)]
        xn = [sb(f"x_norm{i}", [P, TT, D]) for i in range(2)]
        xT = [sb(f"x_normT{i}", [P, DC, TG]) for i in range(2)]
        stats = sb("stats", [P, TT, 6])
        mv = sb("mean_var", [P, TT, 2])
        std = sb("std", [P, TT])
        rstd = sb("rstd", [P, TT])
        piece = [[sb(f"piece{i}_{j}", [P, PIECES, TG], BF16) for j in range(4)] for i in range(2)]
        rest = [sb(f"rest{j}", [P, TG]) for j in range(4)]
        vt = [sb(f"v_tok{i}", [P, TT, H, VC]) for i in range(2)]
        tp = [pb(f"tp{c}", [P, TG]) for c in range(DC)]
        qk = [pb(f"qk{j}", [P, TG]) for j in range(4)]
        vp = [pb(f"vp{i}", [P, 2, D]) for i in range(2)]

        w_loaded = sem("w_loaded")
        x_loaded = [sem(f"x_loaded{i}") for i in range(2)]
        ones_set = sem("ones_set")
        mv_done = sem("mv_done")
        stats_done = sem("stats_done")
        gate = sem("gate")
        std_ready = sem("std_ready")
        eps_added = sem("eps_added")
        rstd_ready = sem("rstd_ready")
        xn_ready = sem("xn_ready")
        transposed = sem("transposed")
        xT_ready = sem("xT_ready")
        qk_ready = sem("qk_ready")
        piece1 = sem("piece1")
        rest_ready = sem("rest_ready")
        piece2 = sem("piece2")
        piece3 = sem("piece3")
        v_ready = sem("v_ready")
        v_evac = sem("v_evac")
        p_stored = [sem(f"p_stored{i}") for i in range(2)]
        v_stored = [sem(f"v_stored{i}") for i in range(2)]
        block = ctx.enter_context(nc.Block())

        @block.sync
        def _(sp):
            for dst, src in zip(w_sb, (wq, wk, wv)):
                sp.dma_start(dst[:], src.rearrange("(c p) n -> p c n", p=P)).then_inc(w_loaded, 16)
            for dst, src in zip(bias, (bq, bk)):
                sp.dma_start(dst[:], src.rearrange("(c p) -> p c", p=P), allow_slow_non_contiguous=True
                             ).then_inc(w_loaded, 16)
            sp.dma_start(bias_v[:], bv.partition_broadcast(P)).then_inc(w_loaded, 16)
            sp.dma_start(ident[:], ident_in).then_inc(w_loaded, 16)
            with sp.Fori(0, B) as b:
                def load(k):
                    if k >= 2:
                        sp.wait_ge(xn_ready, b * GROUPS + (k - 1))
                    sp.dma_start(xt[k % 2][:], x[b, k * TG:(k + 1) * TG, :].rearrange("(t p) d -> p t d", p=P)
                                 ).then_inc(x_loaded[k % 2], 16)
                load(0)
                for k in range(GROUPS):
                    if k + 1 < GROUPS:
                        load(k + 1)
                    cols = slice(k * TG, (k + 1) * TG)
                    for j in range(4):
                        sp.wait_ge(piece3, b * (4 * GROUPS) + (4 * k + j + 1))
                        dst = (qs, ks)[j // 2]
                        for g in range(2):
                            sp.dma_start(dst[b * 4 + (2 * (j % 2) + g)][:, :, cols],
                                         piece[k % 2][j][64 * g:64 * g + 64, :, :]).then_inc(p_stored[k % 2], 16)
                    sp.wait_ge(v_evac, b * (4 * GROUPS) + 4 * (k + 1))
                    for g in range(4):
                        sp.dma_start(vs[b * 4 + g][:, k * TT:(k + 1) * TT, :],
                                     vt[k % 2][:, :, 4 * g:4 * g + 4, :].rearrange("p t h c -> p t (h c)")
                                     ).then_inc(v_stored[k % 2], 16)
            for i in range(2):
                sp.wait_ge(p_stored[i], 16 * 8 * B * GROUPS // 2)
                sp.wait_ge(v_stored[i], 16 * 4 * B * GROUPS // 2)

        @block.vector
        def _(dve):
            for i in range(2):
                nc.vector.memset(vt[i][:, :, :, DK:VC], 0.0).then_inc(ones_set, 1)
            dve.wait_ge(ones_set, 2)
            for i in range(2):
                nc.vector.memset(vt[i][:, :, :, DK:DK + 1], 1.0)
            dve.wait_ge(w_loaded, 16 * 7)
            with dve.Fori(0, B) as b:
                def norm(k):
                    i = k % 2
                    dve.wait_ge(x_loaded[i], b * 32 + 16 * (k // 2 + 1))
                    for t in range(TT):
                        nc.vector.bn_stats(stats[:, t, :], xt[i][:, t, :]).then_inc(stats_done, 1)
                    dve.wait_ge(stats_done, b * (4 * GROUPS) + 4 * (k + 1))
                    nc.vector.nop().then_inc(gate, 1)
                    for t in range(TT):
                        nc.vector.bn_aggr(mv[:, t, :], stats[:, t, :]).then_inc(mv_done, 1)
                    dve.wait_ge(mv_done, b * (4 * GROUPS) + 4 * (k + 1))
                    nc.vector.tensor_scalar_add(std[:], mv[:, :, 1], EPS).then_inc(eps_added, 1)
                    dve.wait_ge(std_ready, b * GROUPS + (k + 1))
                    nc.vector.reciprocal(rstd[:], std[:]).then_inc(rstd_ready, 1)
                    dve.wait_ge(rstd_ready, b * GROUPS + (k + 1))
                    if k >= 2:
                        dve.wait_ge(transposed, b * GROUPS + (k - 1))
                    for t in range(TT):
                        last = nc.vector.tensor_scalar(xn[i][:, t, :], xt[i][:, t, :], mv[:, t, 0:1],
                                                       rstd[:, t:t + 1], ALU.subtract, ALU.mult)
                    last.then_inc(xn_ready, 1)
                norm(0)
                for k in range(GROUPS):
                    for j in range(4):
                        dve.wait_ge(piece1, b * (4 * GROUPS) + (4 * k + j + 1))
                        if k:
                            dve.wait_ge(piece3, b * (4 * GROUPS) + (4 * (k - 1) + j + 1))
                        nc.vector.scalar_tensor_tensor(
                            out=rest[j][:], in0=qk[j][:], scalar=bias[j // 2][:, j % 2:j % 2 + 1],
                            in1=piece[k % 2][j][:, 0, :], op0=ALU.add, op1=ALU.subtract).then_inc(rest_ready, 1)
                    if k + 1 < GROUPS:
                        norm(k + 1)
                    for t in range(TT):
                        dve.wait_ge(v_ready, b * (2 * GROUPS) + (2 * k + t // 2 + 1))
                        if k >= 2 and t == 0:
                            dve.wait_ge(v_stored[k % 2], b * 128 + 64 * (k // 2))
                        nc.vector.tensor_tensor(
                            vt[k % 2][:, t, :, 0:DK], vp[t // 2][:, t % 2, :].rearrange("p (h d) -> p h d", d=DK),
                            bias_v[:].rearrange("p (h d) -> p h d", d=DK), ALU.add).then_inc(v_evac, 1)
                for i in range(2):
                    dve.wait_ge(v_stored[i], b * 128 + 128)
                dve.wait_ge(piece3, b * (4 * GROUPS) + 4 * GROUPS)

        @block.scalar
        def _(act):
            act.wait_ge(w_loaded, 16 * 7)
            with act.Fori(0, B) as b:
                def spread(k):
                    act.wait_ge(eps_added, b * GROUPS + (k + 1))
                    nc.scalar.activation(std[:], std[:], ACT.Sqrt).then_inc(std_ready, 1)

                def copies(k):
                    act.wait_ge(transposed, b * GROUPS + (k + 1))
                    if k >= 2:
                        act.wait_ge(v_ready, b * (2 * GROUPS) + 2 * (k - 1))
                    for c in range(DC):
                        nc.scalar.activation(xT[k % 2][:, c, :], tp[c][:], ACT.Copy).then_inc(xT_ready, 1)
                spread(0)
                copies(0)
                for k in range(GROUPS):
                    def second(j):
                        act.wait_ge(rest_ready, b * (4 * GROUPS) + (4 * k + j + 1))
                        nc.scalar.activation(piece[k % 2][j][:, 1, :], rest[j][:], ACT.Copy).then_inc(piece2, 1)
                    if k >= 2:
                        act.wait_ge(p_stored[k % 2], b * 256 + 128 * (k // 2))
                    for j in range(4):
                        act.wait_ge(qk_ready, b * (4 * GROUPS) + (4 * k + j + 1))
                        nc.scalar.activation(piece[k % 2][j][:, 0, :], qk[j][:], ACT.Identity,
                                             bias=bias[j // 2][:, j % 2:j % 2 + 1]).then_inc(piece1, 1)
                        if j:
                            second(j - 1)
                    second(3)
                    if k + 1 < GROUPS:
                        spread(k + 1)
                        copies(k + 1)
                for i in range(2):
                    act.wait_ge(p_stored[i], b * 256 + 256)
                act.wait_ge(v_ready, b * (2 * GROUPS) + 2 * GROUPS)

        @block.gpsimd
        def _(pool):
            with pool.Fori(0, B) as b:
                for k in range(GROUPS):
                    for j in range(4):
                        pool.wait_ge(piece2, b * (4 * GROUPS) + (4 * k + j + 1))
                        nc.gpsimd.tensor_tensor(piece[k % 2][j][:, 2, :], rest[j][:], piece[k % 2][j][:, 1, :],
                                                ALU.subtract).then_inc(piece3, 1)

        @block.tensor
        def _(pe):
            pe.wait_ge(w_loaded, 16 * 7)
            with pe.Fori(0, B) as b:
                def transposes(k):
                    pe.wait_ge(xn_ready, b * GROUPS + (k + 1))
                    if k:
                        pe.wait_ge(xT_ready, b * (2 * GROUPS) + 2 * k)
                    for c in range(DC):
                        for t in range(TT):
                            last = nc.tensor.transpose(tp[c][:, t * P:(t + 1) * P],
                                                       xn[k % 2][:, t, c * P:(c + 1) * P], ident[:])
                    last.then_inc(transposed, 1)
                transposes(0)
                for k in range(GROUPS):
                    pe.wait_ge(xT_ready, b * (2 * GROUPS) + 2 * (k + 1))
                    for j in range(4):
                        if k:
                            pe.wait_ge(rest_ready, b * (4 * GROUPS) + (4 * (k - 1) + j + 1))
                        for c in range(DC):
                            last = nc.tensor.matmul(qk[j][:], w_sb[j // 2][:, c, (j % 2) * P:(j % 2 + 1) * P],
                                                    xT[k % 2][:, c, :], start=(c == 0), stop=(c == DC - 1))
                        last.then_inc(qk_ready, 1)
                    if k + 1 < GROUPS:
                        transposes(k + 1)
                    for t in range(TT):
                        if k and t % 2 == 0:
                            pe.wait_ge(v_evac, b * (4 * GROUPS) + (4 * (k - 1) + t + 2))
                        for c in range(DC):
                            last = nc.tensor.matmul(vp[t // 2][:, t % 2, :], xT[k % 2][:, c, t * P:(t + 1) * P],
                                                    w_sb[2][:, c, :], start=(c == 0), stop=(c == DC - 1))
                        if t % 2:
                            last.then_inc(v_ready, 1)
                pe.wait_ge(v_evac, b * (4 * GROUPS) + 4 * GROUPS)
                pe.wait_ge(rest_ready, b * (4 * GROUPS) + 4 * GROUPS)
                pe.wait_ge(xT_ready, b * (2 * GROUPS) + 2 * GROUPS)


def attend(nc, tab_add, tab_mul, tab_max, ident_in, qs, ks, vs, ao):
    ctx = ExitStack()
    with ctx:
        sb = lambda n, s, d=F32: ctx.enter_context(nc.sbuf_tensor(n, s, d))
        pb = lambda n, s, d=F32: ctx.enter_context(nc.psum_tensor(n, s, d))
        sem = lambda n: ctx.enter_context(nc.semaphore(n))
        QA = [sb(f"q_slots{i}", [P, GROUPS, HG, TG], BF16) for i in range(2)]
        KA = [sb(f"k_slots{i}", [P, HG, N], BF16) for i in range(2)]
        V = [sb(f"v_heads{i}", [P, KT, HG, VC]) for i in range(2)]
        add_t = sb("decay_add", [P, N])
        mul_t = sb("decay_mul", [P, N - P])
        max_t = sb("decay_max", [P, N])
        ident = sb("ident_b", [P, P])
        identb = sb("ident_bf", [P, P], BF16)
        W = sb("weights", [P, PS, HG, TG])
        junk = sb("junk", [P, 2, 1024], BF16)
        mpart = sb("max_parts", [P, 2, 2, HG * TT])
        mneg = sb("neg_max", [P, 2, 2, HG * TT], BF16)
        mrow = sb("max_rows", [2 * HG * TT, 2, P], BF16)
        ot = [sb(f"out_rows{i}", [P, TG]) for i in range(2)]
        S = [pb(f"scores{i}", [P, TG]) for i in range(SB)]
        M = [pb(f"max_scores{i}", [P, 1024]) for i in range(2)]
        O = pb("attended", [P, TG])

        tables = sem("tables")
        ones_set = sem("ones_set")
        ident_set = sem("ident_set")
        q_loaded = [[sem(f"q_loaded{i}_{c}") for c in range(GROUPS)] for i in range(2)]
        k_loaded = [[sem(f"k_loaded{i}_{c}") for c in range(GROUPS)] for i in range(2)]
        v_loaded = [sem(f"v_loaded{i}") for i in range(2)]
        shift_loaded = [sem(f"shift_loaded{c}") for c in range(GROUPS)]
        scores_ready = sem("scores_ready")
        decayed = sem("decayed")
        exp_done = sem("exp_done")
        weighted = sem("weighted")
        pv_done = sem("pv_done")
        out_copied = sem("out_copied")
        out_stored = [sem(f"out_stored{i}") for i in range(2)]
        max_ready = sem("max_ready")
        max_gate = sem("max_gate")
        max_read = sem("max_read")
        max_joined = sem("max_joined")
        high_ready = sem("high_ready")
        neg_ready = sem("neg_ready")
        slots_loaded = 16 * len(Q_SLOTS)

        block = ctx.enter_context(nc.Block())

        def run(eng, slot):
            for s in range(LAG):
                slot(0, 0, s)
            with eng.Fori(0, NG // 2 - 1) as turn:
                for s in range(LAG, NS):
                    slot(turn, 0, s)
                for s in range(NS):
                    slot(turn, 1, s)
                for s in range(LAG):
                    slot(turn + 1, 0, s)
            for s in range(LAG, NS):
                slot(NG // 2 - 1, 0, s)
            for s in range(NS):
                slot(NG // 2 - 1, 1, s)

        def is_last(turn, parity):
            return isinstance(turn, int) and 2 * turn + parity == NG - 1

        def reloads(turn, parity):
            return not isinstance(turn, int) or 2 * turn + parity < NG - 2

        def before(turn, parity, back):
            return (turn, parity) if not back else (turn, 0) if parity else (turn - 1, 1)

        def exists(turn, parity):
            return not isinstance(turn, int) or turn >= 0

        def count(turn, parity, each, n):
            return turn * (2 * each) + (parity * each + n)

        def wait(eng, semaphore, value):
            if not isinstance(value, int) or value > 0:
                eng.wait_ge(semaphore, value)

        def shifts(turn, parity, s):
            f = finalized(s)
            if f is None or (is_last(turn, parity) and f[0] < GROUPS - 1):
                return None
            if f[0] == GROUPS - 1:
                return (*f, turn, parity)
            return (*f, turn, 1) if parity == 0 else (*f, turn + 1, 0)

        @block.sync
        def _(sp):
            def load_slots(dst, src, which, loaded, c):
                rows = src.rearrange("(h d) w n -> d h w n", d=DK)[:, :, :, c * TG:(c + 1) * TG]
                for n, piece in enumerate(which):
                    sp.dma_start(dst[n * DK:(n + 1) * DK, :, :], rows[:, :, piece, :]).then_inc(loaded, 16)

            def load_q(it, parity, c):
                load_slots(QA[parity][:, c, :, :], qs[it], Q_SLOTS, q_loaded[parity][c], c)

            def load_k(it, parity, c):
                load_slots(KA[parity][:, :, c * TG:(c + 1) * TG], ks[it], K_SLOTS, k_loaded[parity][c], c)

            def load_v(it, parity):
                sp.dma_start(V[parity][:].rearrange("p t h c -> p t (h c)"),
                             vs[it]).then_inc(v_loaded[parity], 16)

            def load_shift(parity, q, read):
                sp.wait_ge(max_read, read)
                for w in range(2):
                    sp.dma_start(QA[parity][KROWS + w:KROWS + w + 1, q, :, :].rearrange("p h (r n) -> p (h r) n", n=P),
                                 mrow[w * HG * TT:(w + 1) * HG * TT, q % 2, :]).then_inc(shift_loaded[q], 16)

            def store_rows(turn, parity, q):
                sp.wait_ge(out_copied, count(turn, parity, GROUPS, q + 1))
                sp.dma_start(ao[turn * 2 + parity][:, q * TG:(q + 1) * TG], ot[q % 2][:]
                             ).then_inc(out_stored[q % 2], 16)

            def slot(turn, parity, s):
                q, j = STEPS[s]
                back, t = trailing(s)
                at = before(turn, parity, back)
                if exists(*at) and t == LAST[STEPS[t][0]]:
                    store_rows(*at, STEPS[t][0])
                    if t == NS - 1 and reloads(*at):
                        load_v(at[0] * 2 + (at[1] + 2), at[1])
                f = shifts(turn, parity, s)
                if f and f[1] == 3:
                    k = ring_start(s + 1, is_last(turn, parity))
                    load_shift(f[3], f[0], count(turn, parity, MAX_ITEMS, MAX_FIRST + k))
                if not reloads(turn, parity):
                    return
                done = count(turn, parity, ITEMS, HG * (s + 1))
                if s == LAST[q]:
                    sp.wait_ge(scores_ready, done)
                    load_q(turn * 2 + (parity + 2), parity, q)
                if q == GROUPS - 1 and j % 4 == 3 and j < 4 * q:
                    sp.wait_ge(scores_ready, done)
                    load_k(turn * 2 + (parity + 2), parity, j // 4)
                if s == NS - 1:
                    load_k(turn * 2 + (parity + 2), parity, GROUPS - 1)

            for c in range(GROUPS):
                load_q(0, 0, c)
                load_k(0, 0, c)
                if c == 0:
                    for dst, src in ((max_t, tab_max), (ident, ident_in), (add_t, tab_add), (mul_t, tab_mul)):
                        sp.dma_start(dst[:], src).then_inc(tables, 16)
            for c in range(GROUPS):
                load_q(1, 1, c)
                load_k(1, 1, c)
            for i in range(2):
                load_v(i, i)
            m = 0
            for what, q, which in opening():
                m += what == "chunk" or which == 3
                if what == "stage" and which == 3:
                    load_shift(0, q, m)
            run(sp, slot)
            store_rows(NG // 2 - 1, 1, GROUPS - 1)
            for i in range(2):
                sp.wait_ge(out_stored[i], 16 * GROUPS * NG // 2)

        @block.tensor
        def _(pe):
            def max_scores(parity, q, chunk, m, bank):
                h, r, _, k0, width = chunk
                wait(pe, max_read, m - 1)
                for c in range(0, width, TG):
                    w = min(TG, width - c)
                    last = nc.tensor.matmul(M[bank][:, c:c + w], QA[parity][0:KROWS, q, h, r * P:(r + 1) * P],
                                            KA[parity][0:KROWS, h, k0 + c:k0 + c + w], start=True, stop=True)
                last.then_inc(max_ready, 1)

            def max_rows(q, ready, m, bank):
                pe.wait_ge(neg_ready, ready)
                wait(pe, max_read, m - 1)
                nc.tensor.transpose(M[bank][0:2 * HG * TT, 0:P // 2].bitcast(BF16),
                                    mneg[:, q % 2, :, :].rearrange("p w c -> p (w c)"), identb[:]
                                    ).then_inc(max_ready, 1)

            def pv(turn, parity, s):
                q, j = STEPS[s]
                if s == 0:
                    pe.wait_ge(v_loaded[parity], turn * 16 + 16)
                if s == FIRST[q]:
                    wait(pe, out_copied, count(turn, parity, GROUPS, q))
                if pool_heads(s):
                    pe.wait_ge(weighted, count(turn, parity, len(POOLED), POOLED.index(s) + 1))
                if pool_heads(s) < HG:
                    pe.wait_ge(exp_done, count(turn, parity, ITEMS, HG * (s + 1)))
                c = first_column(s)
                for h in range(HG):
                    last = nc.tensor.matmul(O[VC * h:VC * (h + 1), c:TG], V[parity][:, j, h, :],
                                            W[:, s % PS, h, c:TG], start=(s == FIRST[q]), stop=(s == LAST[q]),
                                            tile_position=(0, VC * h))
                last.then_inc(pv_done, 1)

            def slot(turn, parity, s):
                q, j = STEPS[s]
                c = first_column(s)
                ahead = not is_last(turn, parity)
                if s == FIRST[q]:
                    if ahead:
                        n = (turn + (1 + parity)) * slots_loaded
                        pe.wait_ge(q_loaded[1 - parity][q], n)
                        pe.wait_ge(k_loaded[1 - parity][q], n)
                    pe.wait_ge(shift_loaded[q], count(turn, parity, 32, 32))
                m = MAX_FIRST + ring_start(s, not ahead)
                for h in range(HG):
                    bank, reuse = score_bank(parity, HG * s + h)
                    wait(pe, exp_done, count(turn, parity, ITEMS, HG * s + h - reuse + 1))
                    nc.tensor.matmul(S[bank][:, c:TG], KA[parity][0:SROWS, h, j * P:(j + 1) * P],
                                     QA[parity][0:SROWS, q, h, c:TG], start=True, stop=True
                                     ).then_inc(scores_ready, 1)
                    for chunk in slot_chunks(s, h) if ahead else ():
                        max_scores(1 - parity, q, chunk, count(turn, parity, MAX_ITEMS, m), m % 2)
                        m += 1
                f = shifts(turn, parity, s)
                if f and f[1] == 3:
                    max_rows(f[0], count(f[2], f[3], GROUPS, f[0] + 1), count(turn, parity, MAX_ITEMS, m), m % 2)
                back, t = trailing(s)
                at = before(turn, parity, back)
                if exists(*at):
                    pv(*at, t)

            pe.wait_ge(tables, 64)
            pe.wait_ge(ident_set, 1)
            m = 0
            for what, q, which in opening():
                if what == "chunk":
                    if which == max_chunks(q)[0]:
                        pe.wait_ge(q_loaded[0][q], slots_loaded)
                        pe.wait_ge(k_loaded[0][q], slots_loaded)
                    max_scores(0, q, which, m, m % 2)
                    m += 1
                elif which == 3:
                    max_rows(q, q + 1, m, m % 2)
                    m += 1
            pe.wait_ge(ones_set, 2)
            run(pe, slot)
            for s in range(NS - LAG, NS):
                pv(NG // 2 - 1, 1, s)

        @block.vector
        def _(dve):
            def maxima(q, chunk, m, bank):
                h, r, part, k0, width = chunk
                dve.wait_ge(max_ready, m + 1)
                if not isinstance(m, int):
                    nc.vector.nop().then_inc(max_gate, 1)
                skew = N - P - P * (TT * q + r) + k0
                nc.vector.tensor_tensor_reduce(
                    out=junk[:, bank, 0:width], in0=M[bank][:, 0:width], in1=max_t[:, skew:skew + width],
                    scale=1.0, scalar=MASKED, op0=ALU.add, op1=ALU.max,
                    accum_out=mpart[:, q % 2, part, h * TT + r:h * TT + r + 1]).then_inc(max_read, 1)

            def stage(q, n, turn, parity, m, bank):
                whole, other = mpart[:, q % 2, 0, :], mpart[:, q % 2, 1, :]
                high, low = mneg[:, q % 2, 0, :], mneg[:, q % 2, 1, :]
                if n == 0:
                    dve.wait_ge(max_read, m)
                    if TG * q + P > 1024:
                        nc.vector.tensor_tensor(whole, whole, other, ALU.max).then_inc(max_joined, 1)
                    else:
                        nc.vector.nop().then_inc(max_joined, 1)
                elif n == 1:
                    dve.wait_ge(max_joined, count(turn, parity, GROUPS, q + 1))
                    nc.vector.tensor_scalar_mul(high, whole, -1.0).then_inc(high_ready, 1)
                elif n == 2:
                    dve.wait_ge(high_ready, count(turn, parity, GROUPS, q + 1))
                    nc.vector.scalar_tensor_tensor(out=low, in0=whole, scalar=-1.0, in1=high,
                                                   op0=ALU.mult, op1=ALU.subtract).then_inc(neg_ready, 1)
                elif n == 3:
                    older = (q - 2, turn, parity) if q >= 2 else (q + 2, *before(turn, parity, 1))
                    wait(dve, shift_loaded[older[0]], count(older[1], older[2], 32, 32))
                    dve.wait_ge(max_ready, m + 1)
                    nc.vector.tensor_copy(mrow[:, q % 2, :], M[bank][0:2 * HG * TT, 0:P // 2].bitcast(BF16)
                                          ).then_inc(max_read, 1)

            def slot(turn, parity, s):
                q, j = STEPS[s]
                c = first_column(s)
                ahead = not is_last(turn, parity)
                m = MAX_FIRST + ring_start(s, not ahead)
                for h in range(HG):
                    if h >= pool_heads(s):
                        dve.wait_ge(scores_ready, count(turn, parity, ITEMS, HG * s + h + 1))
                        bank, _ = score_bank(parity, HG * s + h)
                        x = TG * q + c - P * j
                        nc.vector.tensor_tensor(S[bank][:, c:TG], S[bank][:, c:TG], add_t[:, x:x + TG - c],
                                                ALU.add).then_inc(decayed, 1)
                    for chunk in slot_chunks(s, h) if ahead else ():
                        maxima(q, chunk, count(turn, parity, MAX_ITEMS, m), m % 2)
                        m += 1
                f = shifts(turn, parity, s)
                if f:
                    stage(*f, count(turn, parity, MAX_ITEMS, m), m % 2)

            dve.wait_ge(tables, 64)
            nc.vector.tensor_copy(identb[:], ident[:]).then_inc(ident_set, 1)
            m = 0
            for what, q, which in opening():
                if what == "chunk":
                    maxima(q, which, m, m % 2)
                else:
                    stage(q, which, 0, 0, m, m % 2)
                m += what == "chunk" or which == 3
            run(dve, slot)

        @block.scalar
        def _(act):
            def copy_rows(turn, parity, q):
                act.wait_ge(pv_done, count(turn, parity, NS, LAST[q] + 1))
                wait(act, out_stored[q % 2], count(turn, parity, 32, 16 * (q // 2)))
                nc.scalar.activation(ot[q % 2][:], O[:], ACT.Copy).then_inc(out_copied, 1)

            def slot(turn, parity, s):
                c = first_column(s)
                wait(act, pv_done, count(turn, parity, NS, s - PS + 1))
                for h in range(HG):
                    bank, _ = score_bank(parity, HG * s + h)
                    if h >= pool_heads(s):
                        act.wait_ge(decayed, count(turn, parity, DVE_DECAYS, decay_start(s) + h - pool_heads(s) + 1))
                    else:
                        act.wait_ge(scores_ready, count(turn, parity, ITEMS, HG * s + h + 1))
                    nc.scalar.activation(W[:, s % PS, h, c:TG], S[bank][:, c:TG], ACT.Exp, scale=SCORE_SCALE
                                         ).then_inc(exp_done, 1)
                back, t = trailing(s)
                at = before(turn, parity, back)
                if exists(*at) and t == LAST[STEPS[t][0]]:
                    copy_rows(*at, STEPS[t][0])

            run(act, slot)
            copy_rows(NG // 2 - 1, 1, GROUPS - 1)

        @block.gpsimd
        def _(pool):
            def slot(turn, parity, s):
                q, j = STEPS[s]
                heads = pool_heads(s)
                if heads:
                    pool.wait_ge(exp_done, count(turn, parity, ITEMS, HG * s + heads))
                    w = W[:, s % PS, 0:heads, :]
                    x = TG * q - P * j - P
                    nc.gpsimd.tensor_tensor(w, w, mul_t[:, x:x + TG].unsqueeze(1).to_broadcast([P, heads, TG]),
                                            ALU.mult).then_inc(weighted, 1)

            for i in range(2):
                nc.gpsimd.memset(KA[i][KROWS:SROWS, :, :], 1.0).then_inc(ones_set, 1)
            pool.wait_ge(tables, 64)
            run(pool, slot)


def finish(nc, x, wo, bo, w_gate, w_up, w_down, ident_in, ao, rden, out):
    ctx = ExitStack()
    with ctx:
        sb = lambda n, s, d=F32: ctx.enter_context(nc.sbuf_tensor(n, s, d))
        pb = lambda n, s, d=F32: ctx.enter_context(nc.psum_tensor(n, s, d))
        sem = lambda n: ctx.enter_context(nc.semaphore(n))
        wo_sb = sb("wo_sb", [P, DC, D])
        bias_o = sb("bias_o", [P, D])
        ident = sb("ident_c", [P, P])
        sums = sb("row_sums", [P, N // 2])
        wi = [sb(f"w_int{i}", [P, HC, D], I32) for i in range(2)] + [sb("w_int2", [P, DC, HIDDEN], I32)]
        wf = [sb(f"w_float{i}", [P, HC, D]) for i in range(2)] + [sb("w_float2", [P, DC, HIDDEN])]
        wT = [sb(f"w_inT{i}", [P, DC, HIDDEN]) for i in range(2)]
        dT = sb("w_downT", [P, HC, D])
        num = [sb(f"num{i}", [P, DC, TG]) for i in range(2)]
        rd = [sb(f"rd{i}", [P, DC, TG]) for i in range(2)]
        xt = [sb(f"x_in{i}", [P, TT, D]) for i in range(2)]
        x1 = [sb(f"x_mid{i}", [P, TT, D]) for i in range(2)]
        xn = [sb(f"x_norm2_{i}", [P, TT, D]) for i in range(2)]
        xT = [sb(f"x_norm2T{i}", [P, DC, TG]) for i in range(2)]
        hT = sb("hiddenT", [P, HC, TG])
        sg = [sb(f"silu{i}", [P, TG]) for i in range(2)]
        y = [sb(f"y{i}", [P, TT, D]) for i in range(2)]
        stats = sb("stats2", [P, TT, 6])
        mv = sb("mean_var2", [P, TT, 2])
        std = sb("std2", [P, TT])
        rstd = sb("rstd2", [P, TT])
        wo_ps = [pb(f"wo_ps{i}", [P, TG]) for i in range(2)]
        dn_ps = [pb(f"dn_ps{i}", [P, TG]) for i in range(2)]
        g_ps = [pb(f"g_ps{i}", [P, TG]) for i in range(2)]
        u_ps = [pb(f"u_ps{i}", [P, TG]) for i in range(2)]

        consts = sem("consts")
        sums_in = sem("sums_in")
        inverted = sem("inverted")
        rden_out = sem("rden_out")
        cast = sem("w_cast")
        w_turned = sem("w_turned")
        w_copied = sem("w_copied")
        loaded = [sem(f"c_loaded{i}") for i in range(2)]
        biased = sem("biased")
        a_ready = sem("a_ready")
        wo_done = sem("wo_done")
        x1_ready = sem("x1_ready")
        mv_done = sem("mv_done2")
        stats_done = sem("stats_done2")
        gate = sem("gate2")
        eps_added = sem("eps_added2")
        std_ready = sem("std_ready2")
        rstd_ready = sem("rstd_ready2")
        xn_ready = sem("xn_ready2")
        transposed = sem("transposed2")
        xT_ready = sem("xT_ready2")
        gu_ready = sem("gu_ready")
        silu_ready = sem("silu_ready")
        h_ready = sem("h_ready")
        down_ready = sem("down_ready")
        y_ready = sem("y_ready")
        stored = [sem(f"stored{i}") for i in range(2)]
        block = ctx.enter_context(nc.Block())
        ao_rows = ao.rearrange("g (h r) n -> (g h) r n", r=VC)

        @block.sync
        def _(sp):
            sp.dma_start(sums[:], ao_rows[:, DK, :].rearrange("h (a n) -> h a n", a=2)).then_inc(sums_in, 16)
            for dst, src in zip(wi, (w_gate, w_up, w_down)):
                sp.dma_start(dst[:], src.rearrange("(c p) n -> p c n", p=P)).then_inc(consts, 16)
            sp.dma_start(wo_sb[:], wo.rearrange("(c p) n -> p c n", p=P)).then_inc(consts, 16)
            sp.dma_start(bias_o[:], bo.partition_broadcast(P)).then_inc(consts, 16)
            sp.dma_start(ident[:], ident_in).then_inc(consts, 16)
            sp.wait_ge(inverted, 1)
            sp.dma_start(rden.rearrange("h (a n) -> h a n", a=2), sums[:]).then_inc(rden_out, 16)
            sp.wait_ge(rden_out, 16)
            with sp.Fori(0, B) as b:
                def load(k):
                    i, cols = k % 2, slice(k * TG, (k + 1) * TG)
                    if k >= 2:
                        sp.wait_ge(x1_ready, b * (4 * GROUPS) + 4 * (k - 1))
                    for c in range(DC):
                        heads = ao_rows.rearrange("(b c h) r n -> b c h r n", b=B, c=DC)[b][c]
                        recips = rden.rearrange("(b c h) n -> b c h n", b=B, c=DC)[b][c]
                        sp.dma_start(num[i][:, c, :], heads[:, 0:DK, cols]).then_inc(loaded[i], 16)
                        sp.dma_start(rd[i][:, c, :], recips[:, cols].unsqueeze(1).to_broadcast([H // DC, DK, TG])
                                     ).then_inc(loaded[i], 16)
                    sp.dma_start(xt[i][:], x[b, cols, :].rearrange("(t p) d -> p t d", p=P)).then_inc(loaded[i], 16)
                load(0)
                for k in range(GROUPS):
                    if k + 1 < GROUPS:
                        load(k + 1)
                    sp.wait_ge(y_ready, b * (4 * GROUPS) + 4 * (k + 1))
                    sp.dma_start(out[b, k * TG:(k + 1) * TG, :].rearrange("(t p) d -> p t d", p=P), y[k % 2][:]
                                 ).then_inc(stored[k % 2], 16)
            for i in range(2):
                sp.wait_ge(stored[i], 16 * B * GROUPS // 2)

        @block.gpsimd
        def _(pool):
            pool.wait_ge(consts, 16 * 6)
            with pool.Fori(0, B) as b:
                for k in range(GROUPS):
                    i = k % 2
                    pool.wait_ge(loaded[i], b * 160 + 80 * (k // 2 + 1))
                    for t in range(TT):
                        last = nc.gpsimd.tensor_tensor(xt[i][:, t, :], xt[i][:, t, :], bias_o[:], ALU.add)
                    last.then_inc(biased, 1)

        @block.vector
        def _(dve):
            dve.wait_ge(sums_in, 16)
            nc.vector.reciprocal(sums[:], sums[:]).then_inc(inverted, 1)
            dve.wait_ge(consts, 16 * 6)
            for i in range(3):
                nc.vector.tensor_copy(wf[i][:], wi[i][:]).then_inc(cast, 1)
            with dve.Fori(0, B) as b:
                def attended(k):
                    i = k % 2
                    dve.wait_ge(loaded[i], b * 160 + 80 * (k // 2 + 1))
                    nc.vector.tensor_tensor(num[i][:], num[i][:], rd[i][:], ALU.mult).then_inc(a_ready, 1)

                def norm(k):
                    i = k % 2
                    dve.wait_ge(biased, b * GROUPS + (k + 1))
                    for t in range(TT):
                        if t % 2 == 0:
                            dve.wait_ge(wo_done, b * (2 * GROUPS) + (2 * k + t // 2 + 1))
                        nc.vector.tensor_tensor(x1[i][:, t, :], wo_ps[t // 2][:, (t % 2) * D:(t % 2 + 1) * D],
                                                xt[i][:, t, :], ALU.add).then_inc(x1_ready, 1)
                    for t in range(TT):
                        if t == 0:
                            dve.wait_ge(x1_ready, b * (4 * GROUPS) + 4 * (k + 1))
                        nc.vector.bn_stats(stats[:, t, :], x1[i][:, t, :]).then_inc(stats_done, 1)
                    dve.wait_ge(stats_done, b * (4 * GROUPS) + 4 * (k + 1))
                    nc.vector.nop().then_inc(gate, 1)
                    for t in range(TT):
                        nc.vector.bn_aggr(mv[:, t, :], stats[:, t, :]).then_inc(mv_done, 1)
                    dve.wait_ge(mv_done, b * (4 * GROUPS) + 4 * (k + 1))
                    nc.vector.tensor_scalar_add(std[:], mv[:, :, 1], EPS).then_inc(eps_added, 1)
                    dve.wait_ge(std_ready, b * GROUPS + (k + 1))
                    nc.vector.reciprocal(rstd[:], std[:]).then_inc(rstd_ready, 1)
                    dve.wait_ge(rstd_ready, b * GROUPS + (k + 1))
                    for t in range(TT):
                        last = nc.vector.tensor_scalar(xn[i][:, t, :], x1[i][:, t, :], mv[:, t, 0:1],
                                                       rstd[:, t:t + 1], ALU.subtract, ALU.mult)
                    last.then_inc(xn_ready, 1)

                attended(0)
                norm(0)
                for k in range(GROUPS):
                    if k + 1 < GROUPS:
                        attended(k + 1)
                    if k:
                        dve.wait_ge(down_ready, b * (2 * GROUPS) + 2 * k)
                    for m in range(HC):
                        dve.wait_ge(silu_ready, b * (HC * GROUPS) + (HC * k + m + 1))
                        nc.vector.scalar_tensor_tensor(out=hT[:, m, :], in0=u_ps[m % 2][:], scalar=W_SCALE,
                                                       in1=sg[m % 2][:], op0=ALU.mult, op1=ALU.mult
                                                       ).then_inc(h_ready, 1)
                    if k + 1 < GROUPS:
                        norm(k + 1)
                    if k >= 2:
                        dve.wait_ge(stored[k % 2], b * 32 + 16 * (k // 2))
                    for t in range(TT):
                        if t % 2 == 0:
                            dve.wait_ge(down_ready, b * (2 * GROUPS) + (2 * k + t // 2 + 1))
                        nc.vector.scalar_tensor_tensor(
                            out=y[k % 2][:, t, :], in0=dn_ps[t // 2][:, (t % 2) * D:(t % 2 + 1) * D],
                            scalar=W_SCALE, in1=x1[k % 2][:, t, :], op0=ALU.mult, op1=ALU.add).then_inc(y_ready, 1)
                for i in range(2):
                    dve.wait_ge(stored[i], b * 32 + 32)

        @block.scalar
        def _(act):
            n = 0
            for i in range(3):
                for c in range(DC if i < 2 else HC):
                    for part in range(2 if i < 2 else 1):
                        w = (TG, HIDDEN - TG)[part] if i < 2 else D
                        act.wait_ge(w_turned, n + 1)
                        dst = wT[i][:, c, part * TG:part * TG + w] if i < 2 else dT[:, c, :]
                        nc.scalar.activation(dst, g_ps[n % 2][:, 0:w], ACT.Copy).then_inc(w_copied, 1)
                        n += 1
            with act.Fori(0, B) as b:
                def root_and_copies(k):
                    act.wait_ge(eps_added, b * GROUPS + (k + 1))
                    nc.scalar.activation(std[:], std[:], ACT.Sqrt).then_inc(std_ready, 1)
                    act.wait_ge(transposed, b * GROUPS + (k + 1))
                    for c in range(DC):
                        nc.scalar.activation(xT[k % 2][:, c, :], dn_ps[c][:], ACT.Copy).then_inc(xT_ready, 1)
                root_and_copies(0)
                for k in range(GROUPS):
                    for m in range(HC):
                        act.wait_ge(gu_ready, b * (HC * GROUPS) + (HC * k + m + 1))
                        if k or m >= 2:
                            act.wait_ge(h_ready, b * (HC * GROUPS) + (HC * k + m - 1))
                        nc.scalar.activation(sg[m % 2][:], g_ps[m % 2][:], ACT.Silu, scale=W_SCALE
                                             ).then_inc(silu_ready, 1)
                    if k + 1 < GROUPS:
                        root_and_copies(k + 1)
                act.wait_ge(h_ready, b * (HC * GROUPS) + HC * GROUPS)

        @block.tensor
        def _(pe):
            pe.wait_ge(consts, 16 * 6)
            n = 0
            for i in range(3):
                pe.wait_ge(cast, i + 1)
                for c in range(DC if i < 2 else HC):
                    for part in range(2 if i < 2 else 1):
                        w = (TG, HIDDEN - TG)[part] if i < 2 else D
                        if n >= 2:
                            pe.wait_ge(w_copied, n - 1)
                        for a in range(w // P):
                            src = (wf[i][:, part * TT + a, c * P:(c + 1) * P] if i < 2
                                   else wf[i][:, a, c * P:(c + 1) * P])
                            last = nc.tensor.transpose(g_ps[n % 2][:, a * P:(a + 1) * P], src, ident[:])
                        last.then_inc(w_turned, 1)
                        n += 1
            pe.wait_ge(w_copied, n)
            with pe.Fori(0, B) as b:
                def out_proj(k):
                    pe.wait_ge(a_ready, b * GROUPS + (k + 1))
                    if k:
                        pe.wait_ge(x1_ready, b * (4 * GROUPS) + 4 * k)
                    for t in range(TT):
                        for c in range(DC):
                            last = nc.tensor.matmul(wo_ps[t // 2][:, (t % 2) * D:(t % 2 + 1) * D],
                                                    num[k % 2][:, c, t * P:(t + 1) * P], wo_sb[:, c, :],
                                                    start=(c == 0), stop=(c == DC - 1))
                        if t % 2:
                            last.then_inc(wo_done, 1)

                def transposes(k):
                    pe.wait_ge(xn_ready, b * GROUPS + (k + 1))
                    if k:
                        pe.wait_ge(y_ready, b * (4 * GROUPS) + 4 * k)
                    for c in range(DC):
                        for t in range(TT):
                            last = nc.tensor.transpose(dn_ps[c][:, t * P:(t + 1) * P],
                                                       xn[k % 2][:, t, c * P:(c + 1) * P], ident[:])
                    last.then_inc(transposed, 1)

                out_proj(0)
                transposes(0)
                for k in range(GROUPS):
                    pe.wait_ge(xT_ready, b * (2 * GROUPS) + 2 * (k + 1))
                    for m in range(HC):
                        if k or m >= 2:
                            pe.wait_ge(h_ready, b * (HC * GROUPS) + (HC * k + m - 1))
                        for w, ps in ((wT[0], g_ps), (wT[1], u_ps)):
                            for c in range(DC):
                                last = nc.tensor.matmul(ps[m % 2][:], w[:, c, m * P:(m + 1) * P], xT[k % 2][:, c, :],
                                                        start=(c == 0), stop=(c == DC - 1))
                        last.then_inc(gu_ready, 1)
                    if k + 1 < GROUPS:
                        out_proj(k + 1)
                    pe.wait_ge(h_ready, b * (HC * GROUPS) + HC * (k + 1))
                    for t in range(TT):
                        for m in range(HC):
                            last = nc.tensor.matmul(dn_ps[t // 2][:, (t % 2) * D:(t % 2 + 1) * D],
                                                    hT[:, m, t * P:(t + 1) * P], dT[:, m, :],
                                                    start=(m == 0), stop=(m == HC - 1))
                        if t % 2:
                            last.then_inc(down_ready, 1)
                    if k + 1 < GROUPS:
                        transposes(k + 1)
                pe.wait_ge(y_ready, b * (4 * GROUPS) + 4 * GROUPS)
                pe.wait_ge(x1_ready, b * (4 * GROUPS) + 4 * GROUPS)


def build(nc, x, wq, bq, wk, bk, wv, bv, wo, bo, w_gate, w_up, w_down, tab_add, tab_mul, tab_max, ident, out):
    def scratch(name, shape, dtype=F32):
        return nc.dram_tensor(name, shape, dtype, kind="Internal").ap()
    qs = scratch("q_pieces", (NG, RG, PIECES, N), BF16)
    ks = scratch("k_pieces", (NG, RG, PIECES, N), BF16)
    vs = scratch("v_ones", (NG, P, KT, HG * VC))
    ao = scratch("attn_rows", (NG, HG * VC, N))
    rden = scratch("row_reciprocals", (B * H, N))
    project(nc, x, wq, bq, wk, bk, wv, bv, ident, qs, ks, vs)
    attend(nc, tab_add, tab_mul, tab_max, ident, qs, ks, vs, ao)
    finish(nc, x, wo, bo, w_gate, w_up, w_down, ident, ao, rden, out)


def decay_tables():
    key, col = np.arange(P)[:, None], np.arange(N)[None, :]

    def added(distance):
        log = -DECAY * np.log(np.maximum(distance, 1).astype(np.float64)) / SCORE_SCALE
        return np.where(distance < 0, MASKED, log).astype(np.float32)
    mul = (col[:, :N - P] + P - key).astype(np.float64) ** -DECAY
    return added(col - key), mul.astype(np.float32), added(key - (col - (N - P)))


def kernel(**inputs):
    import concourse.bacc as bacc
    from concourse.bass_utils import run_bass_kernel_spmd

    nc = bacc.Bacc("TRN2", target_bir_lowering=False, num_devices=1)
    names = ["L0_attn_" + n for n in ("x", "Wq", "bq", "Wk", "bk", "Wv", "bv", "Wo", "bo")]
    names += ["L0_ffn_" + n for n in ("w_gate", "w_up", "w_down")]
    arrays = {n: np.ascontiguousarray(inputs[n]) for n in names}
    arrays |= dict(zip(("decay_add_t", "decay_mul_t", "decay_max_t"), decay_tables()))
    arrays["identity"] = np.eye(P, dtype=np.float32)
    args = [nc.dram_tensor(n, a.shape, mybir.dt.from_np(a.dtype), kind="ExternalInput").ap()
            for n, a in arrays.items()]
    out = nc.dram_tensor("out", (B, N, D), F32, kind="ExternalOutput").ap()
    build(nc, *args, out)
    return run_bass_kernel_spmd(nc, [arrays], core_ids=[0]).results[0]["out"]
```

```python
import math
from contextlib import ExitStack

import numpy as np

import concourse.bass as bass
from concourse import mybir

P = 128
B, N, D = 4, 2048, 256
H = 16
DK = D // H
HIDDEN = 768
EPS = 1e-5
DECAY = 0.25
W_SCALE = 1.0 / 127.0
SCORE_SCALE = 1.0 / math.sqrt(DK)
MASKED = -3.0e38

TG = 512
GROUPS = N // TG
DC = D // P
HC = HIDDEN // P
TT = TG // P
HG = 4
NG = B * H // HG
RG = HG * DK
PIECES = 3
Q_SLOTS = (0, 1, 2, 0, 1, 0)
K_SLOTS = (0, 0, 0, 1, 1, 2)
KROWS = len(Q_SLOTS) * DK
SROWS = KROWS + 2
VC = 32
KT = N // P

F32 = mybir.dt.float32
BF16 = mybir.dt.bfloat16
I32 = mybir.dt.int32
ALU = mybir.AluOpType
ACT = mybir.ActivationFunctionType

ADVANCE = 2
CUT = 17
DECAY_LAG = 1
LAG = 5
PS = 8
EAGER = 1.05
POOL_FULL = (3, 3)
POOL_DIAGONAL = (3, 3, 3, 3)


def key_tiles(q):
    full, diagonal = list(range(4 * q)), list(range(4 * q, 4 * q + 4))
    return [j for i in range(4) for j in full[i * q:(i + 1) * q] + [diagonal[i]]]


STEPS = [(q, j) for q in range(GROUPS) for j in key_tiles(q)]
NS = len(STEPS)
FIRST = [STEPS.index((q, key_tiles(q)[0])) for q in range(GROUPS)]
LAST = [STEPS.index((q, key_tiles(q)[-1])) for q in range(GROUPS)]


def pool_heads(s):
    q, j = STEPS[s]
    return POOL_DIAGONAL[j - 4 * q] if j >= 4 * q else POOL_FULL[s % 2]


POOLED = [s for s in range(NS) if pool_heads(s)]
SHARED = [s for s in range(NS) if pool_heads(s) < HG]
SB = 3
ITEMS = HG * NS


def first_column(s):
    q, j = STEPS[s]
    return P * max(0, j - 4 * q)


def score_bank(parity, n):
    i = ITEMS * parity + n
    back = SB
    if i < SB:
        last = max(k for k in range(2 * ITEMS) if k % SB == i % SB)
        back = 2 * ITEMS + i - last
    return i % SB, back


def max_chunks(q):
    out = []
    for h in range(HG):
        for r in range(TT):
            width = TG * q + P * (r + 1)
            for part in range((width + 1023) // 1024):
                out.append((h, r, part, 1024 * part, min(1024, width - 1024 * part)))
    return out


def plan_maxima():
    ring, stages = [None] * ITEMS, [[] for _ in range(ITEMS)]
    chunks = [("chunk", q, chunk) for q in range(GROUPS) for chunk in max_chunks(q)]
    share = EAGER * sum(c[2][4] for c in chunks) / (HG * sum(TG - first_column(s) for s in range(NS)))
    due = 0.0
    for x in range(ADVANCE, ITEMS):
        due += share * (TG - first_column(x // HG))
        if chunks and due > 0:
            ring[x] = chunks.pop(0)
            due -= ring[x][2][4]
    assert not chunks
    for q in range(GROUPS):
        last = q == GROUPS - 1
        end = ITEMS - 1 if last else max(x for x in range(ITEMS) if ring[x] and ring[x][:2] == ("chunk", q))
        for n in range(3):
            x = end + 1 + 2 * n
            stages[x % ITEMS].append((q, n, last))
        x = end + 6 + ADVANCE
        while ring[x % ITEMS]:
            x += 1
        assert last == (x >= ITEMS)
        ring[x % ITEMS] = ("rows", q, last)
    assert not any(ring[:ADVANCE])
    return ring, stages


RING, STAGES = plan_maxima()


def in_ring(x, last):
    what = RING[x] if x < ITEMS else None
    return what if what and (not last or (what[0] == "rows" and what[2])) else None


def ring_count(x, last):
    return sum(in_ring(y, last) is not None for y in range(x))


def opening():
    for q in range(GROUPS):
        for i, chunk in enumerate(max_chunks(q)):
            yield "chunk", q, chunk
            if q and i % 2 and i // 2 < 4:
                yield "stage", q - 1, i // 2


MAX_ITEMS = sum(len(max_chunks(q)) for q in range(GROUPS)) + GROUPS
MAX_FIRST = MAX_ITEMS - 1


def delayed(s, lag):
    return (0, s - lag) if s >= lag else (1, s - lag + NS)


def project(nc, x, wq, bq, wk, bk, wv, bv, ident_in, qs, ks, vs):
    ctx = ExitStack()
    with ctx:
        sb = lambda n, s, d=F32: ctx.enter_context(nc.sbuf_tensor(n, s, d))
        pb = lambda n, s, d=F32: ctx.enter_context(nc.psum_tensor(n, s, d))
        sem = lambda n: ctx.enter_context(nc.semaphore(n))
        w_sb = [sb(f"w_{n}", [P, DC, D]) for n in "qkv"]
        bias = [sb(f"bias_{n}", [P, DC]) for n in "qk"]
        bias_v = sb("bias_v", [P, D])
        ident = sb("ident_a", [P, P])
        xt = [sb(f"x_tok{i}", [P, TT, D]) for i in range(2)]
        xn = [sb(f"x_norm{i}", [P, TT, D]) for i in range(2)]
        xT = [sb(f"x_normT{i}", [P, DC, TG]) for i in range(2)]
        stats = sb("stats", [P, TT, 6])
        mv = sb("mean_var", [P, TT, 2])
        std = sb("std", [P, TT])
        rstd = sb("rstd", [P, TT])
        piece = [[sb(f"piece{i}_{j}", [P, PIECES, TG], BF16) for j in range(4)] for i in range(2)]
        rest = [sb(f"rest{j}", [P, TG]) for j in range(4)]
        vt = [sb(f"v_tok{i}", [P, TT, H, VC]) for i in range(2)]
        tp = [pb(f"tp{c}", [P, TG]) for c in range(DC)]
        qk = [pb(f"qk{j}", [P, TG]) for j in range(4)]
        vp = [pb(f"vp{i}", [P, 2, D]) for i in range(2)]

        w_loaded = sem("w_loaded")
        x_loaded = [sem(f"x_loaded{i}") for i in range(2)]
        ones_set = sem("ones_set")
        mv_done = sem("mv_done")
        stats_done = sem("stats_done")
        gate = sem("gate")
        std_ready = sem("std_ready")
        eps_added = sem("eps_added")
        rstd_ready = sem("rstd_ready")
        xn_ready = sem("xn_ready")
        transposed = sem("transposed")
        xT_ready = sem("xT_ready")
        qk_ready = sem("qk_ready")
        piece1 = sem("piece1")
        rest_ready = sem("rest_ready")
        piece2 = sem("piece2")
        piece3 = sem("piece3")
        v_ready = sem("v_ready")
        v_evac = sem("v_evac")
        p_stored = [sem(f"p_stored{i}") for i in range(2)]
        v_stored = [sem(f"v_stored{i}") for i in range(2)]
        block = ctx.enter_context(nc.Block())

        @block.sync
        def _(sp):
            for dst, src in zip(w_sb, (wq, wk, wv)):
                sp.dma_start(dst[:], src.rearrange("(c p) n -> p c n", p=P)).then_inc(w_loaded, 16)
            for dst, src in zip(bias, (bq, bk)):
                sp.dma_start(dst[:], src.rearrange("(c p) -> p c", p=P), allow_slow_non_contiguous=True
                             ).then_inc(w_loaded, 16)
            sp.dma_start(bias_v[:], bv.partition_broadcast(P)).then_inc(w_loaded, 16)
            sp.dma_start(ident[:], ident_in).then_inc(w_loaded, 16)
            with sp.Fori(0, B) as b:
                def load(k):
                    if k >= 2:
                        sp.wait_ge(xn_ready, b * GROUPS + (k - 1))
                    sp.dma_start(xt[k % 2][:], x[b, k * TG:(k + 1) * TG, :].rearrange("(t p) d -> p t d", p=P)
                                 ).then_inc(x_loaded[k % 2], 16)
                load(0)
                for k in range(GROUPS):
                    if k + 1 < GROUPS:
                        load(k + 1)
                    cols = slice(k * TG, (k + 1) * TG)
                    for j in range(4):
                        sp.wait_ge(piece3, b * (4 * GROUPS) + (4 * k + j + 1))
                        dst = (qs, ks)[j // 2]
                        for g in range(2):
                            sp.dma_start(dst[b * 4 + (2 * (j % 2) + g)][:, :, cols],
                                         piece[k % 2][j][64 * g:64 * g + 64, :, :]).then_inc(p_stored[k % 2], 16)
                    sp.wait_ge(v_evac, b * (4 * GROUPS) + 4 * (k + 1))
                    for g in range(4):
                        sp.dma_start(vs[b * 4 + g][:, k * TT:(k + 1) * TT, :],
                                     vt[k % 2][:, :, 4 * g:4 * g + 4, :].rearrange("p t h c -> p t (h c)")
                                     ).then_inc(v_stored[k % 2], 16)
            for i in range(2):
                sp.wait_ge(p_stored[i], 16 * 8 * B * GROUPS // 2)
                sp.wait_ge(v_stored[i], 16 * 4 * B * GROUPS // 2)

        @block.vector
        def _(dve):
            for i in range(2):
                nc.vector.memset(vt[i][:, :, :, DK:VC], 0.0).then_inc(ones_set, 1)
            dve.wait_ge(ones_set, 2)
            for i in range(2):
                nc.vector.memset(vt[i][:, :, :, DK:DK + 1], 1.0)
            dve.wait_ge(w_loaded, 16 * 7)
            with dve.Fori(0, B) as b:
                def norm(k):
                    i = k % 2
                    dve.wait_ge(x_loaded[i], b * 32 + 16 * (k // 2 + 1))
                    for t in range(TT):
                        nc.vector.bn_stats(stats[:, t, :], xt[i][:, t, :]).then_inc(stats_done, 1)
                    dve.wait_ge(stats_done, b * (4 * GROUPS) + 4 * (k + 1))
                    nc.vector.nop().then_inc(gate, 1)
                    for t in range(TT):
                        nc.vector.bn_aggr(mv[:, t, :], stats[:, t, :]).then_inc(mv_done, 1)
                    dve.wait_ge(mv_done, b * (4 * GROUPS) + 4 * (k + 1))
                    nc.vector.tensor_scalar_add(std[:], mv[:, :, 1], EPS).then_inc(eps_added, 1)
                    dve.wait_ge(std_ready, b * GROUPS + (k + 1))
                    nc.vector.reciprocal(rstd[:], std[:]).then_inc(rstd_ready, 1)
                    dve.wait_ge(rstd_ready, b * GROUPS + (k + 1))
                    if k >= 2:
                        dve.wait_ge(transposed, b * GROUPS + (k - 1))
                    for t in range(TT):
                        last = nc.vector.tensor_scalar(xn[i][:, t, :], xt[i][:, t, :], mv[:, t, 0:1],
                                                       rstd[:, t:t + 1], ALU.subtract, ALU.mult)
                    last.then_inc(xn_ready, 1)
                norm(0)
                for k in range(GROUPS):
                    for j in range(4):
                        dve.wait_ge(piece1, b * (4 * GROUPS) + (4 * k + j + 1))
                        if k:
                            dve.wait_ge(piece3, b * (4 * GROUPS) + (4 * (k - 1) + j + 1))
                        nc.vector.scalar_tensor_tensor(
                            out=rest[j][:], in0=qk[j][:], scalar=bias[j // 2][:, j % 2:j % 2 + 1],
                            in1=piece[k % 2][j][:, 0, :], op0=ALU.add, op1=ALU.subtract).then_inc(rest_ready, 1)
                    if k + 1 < GROUPS:
                        norm(k + 1)
                    for t in range(TT):
                        dve.wait_ge(v_ready, b * (2 * GROUPS) + (2 * k + t // 2 + 1))
                        if k >= 2 and t == 0:
                            dve.wait_ge(v_stored[k % 2], b * 128 + 64 * (k // 2))
                        nc.vector.tensor_tensor(
                            vt[k % 2][:, t, :, 0:DK], vp[t // 2][:, t % 2, :].rearrange("p (h d) -> p h d", d=DK),
                            bias_v[:].rearrange("p (h d) -> p h d", d=DK), ALU.add).then_inc(v_evac, 1)
                for i in range(2):
                    dve.wait_ge(v_stored[i], b * 128 + 128)
                dve.wait_ge(piece3, b * (4 * GROUPS) + 4 * GROUPS)

        @block.scalar
        def _(act):
            act.wait_ge(w_loaded, 16 * 7)
            with act.Fori(0, B) as b:
                def spread(k):
                    act.wait_ge(eps_added, b * GROUPS + (k + 1))
                    nc.scalar.activation(std[:], std[:], ACT.Sqrt).then_inc(std_ready, 1)

                def copies(k):
                    act.wait_ge(transposed, b * GROUPS + (k + 1))
                    if k >= 2:
                        act.wait_ge(v_ready, b * (2 * GROUPS) + 2 * (k - 1))
                    for c in range(DC):
                        nc.scalar.activation(xT[k % 2][:, c, :], tp[c][:], ACT.Copy).then_inc(xT_ready, 1)
                spread(0)
                copies(0)
                for k in range(GROUPS):
                    def second(j):
                        act.wait_ge(rest_ready, b * (4 * GROUPS) + (4 * k + j + 1))
                        nc.scalar.activation(piece[k % 2][j][:, 1, :], rest[j][:], ACT.Copy).then_inc(piece2, 1)
                    if k >= 2:
                        act.wait_ge(p_stored[k % 2], b * 256 + 128 * (k // 2))
                    for j in range(4):
                        act.wait_ge(qk_ready, b * (4 * GROUPS) + (4 * k + j + 1))
                        nc.scalar.activation(piece[k % 2][j][:, 0, :], qk[j][:], ACT.Identity,
                                             bias=bias[j // 2][:, j % 2:j % 2 + 1]).then_inc(piece1, 1)
                        if j:
                            second(j - 1)
                    second(3)
                    if k + 1 < GROUPS:
                        spread(k + 1)
                        copies(k + 1)
                for i in range(2):
                    act.wait_ge(p_stored[i], b * 256 + 256)
                act.wait_ge(v_ready, b * (2 * GROUPS) + 2 * GROUPS)

        @block.gpsimd
        def _(pool):
            with pool.Fori(0, B) as b:
                for k in range(GROUPS):
                    for j in range(4):
                        pool.wait_ge(piece2, b * (4 * GROUPS) + (4 * k + j + 1))
                        nc.gpsimd.tensor_tensor(piece[k % 2][j][:, 2, :], rest[j][:], piece[k % 2][j][:, 1, :],
                                                ALU.subtract).then_inc(piece3, 1)

        @block.tensor
        def _(pe):
            pe.wait_ge(w_loaded, 16 * 7)
            with pe.Fori(0, B) as b:
                def transposes(k):
                    pe.wait_ge(xn_ready, b * GROUPS + (k + 1))
                    if k:
                        pe.wait_ge(xT_ready, b * (2 * GROUPS) + 2 * k)
                    for c in range(DC):
                        for t in range(TT):
                            last = nc.tensor.transpose(tp[c][:, t * P:(t + 1) * P],
                                                       xn[k % 2][:, t, c * P:(c + 1) * P], ident[:])
                    last.then_inc(transposed, 1)
                transposes(0)
                for k in range(GROUPS):
                    pe.wait_ge(xT_ready, b * (2 * GROUPS) + 2 * (k + 1))
                    for j in range(4):
                        if k:
                            pe.wait_ge(rest_ready, b * (4 * GROUPS) + (4 * (k - 1) + j + 1))
                        for c in range(DC):
                            last = nc.tensor.matmul(qk[j][:], w_sb[j // 2][:, c, (j % 2) * P:(j % 2 + 1) * P],
                                                    xT[k % 2][:, c, :], start=(c == 0), stop=(c == DC - 1))
                        last.then_inc(qk_ready, 1)
                    if k + 1 < GROUPS:
                        transposes(k + 1)
                    for t in range(TT):
                        if k and t % 2 == 0:
                            pe.wait_ge(v_evac, b * (4 * GROUPS) + (4 * (k - 1) + t + 2))
                        for c in range(DC):
                            last = nc.tensor.matmul(vp[t // 2][:, t % 2, :], xT[k % 2][:, c, t * P:(t + 1) * P],
                                                    w_sb[2][:, c, :], start=(c == 0), stop=(c == DC - 1))
                        if t % 2:
                            last.then_inc(v_ready, 1)
                pe.wait_ge(v_evac, b * (4 * GROUPS) + 4 * GROUPS)
                pe.wait_ge(rest_ready, b * (4 * GROUPS) + 4 * GROUPS)
                pe.wait_ge(xT_ready, b * (2 * GROUPS) + 2 * GROUPS)


def attend(nc, mask_kq, mask_qk, tab_mul, ident_in, qs, ks, vs, ao):
    ctx = ExitStack()
    with ctx:
        sb = lambda n, s, d=F32: ctx.enter_context(nc.sbuf_tensor(n, s, d))
        pb = lambda n, s, d=F32: ctx.enter_context(nc.psum_tensor(n, s, d))
        sem = lambda n: ctx.enter_context(nc.semaphore(n))
        QA = [sb(f"q_slots{i}", [P, GROUPS, HG, TG], BF16) for i in range(2)]
        KA = [sb(f"k_slots{i}", [P, HG, N], BF16) for i in range(2)]
        V = [sb(f"v_heads{i}", [P, KT, HG, VC]) for i in range(2)]
        mul_t = sb("decay_mul", [P, N])
        ident = sb("ident_b", [P, P])
        identb = sb("ident_bf", [P, P], BF16)
        mask_in = [sb(f"mask_f{i}", [P, P]) for i in range(2)]
        mask = [sb(f"mask_bf{i}", [P, P], BF16) for i in range(2)]
        W = sb("weights", [P, PS, HG, TG])
        mpart = sb("max_parts", [P, 2, 2, HG * TT])
        mneg = sb("neg_max", [P, 2, 2, HG * TT], BF16)
        mrow = sb("max_rows", [2 * HG * TT, 2, P], BF16)
        ot = [sb(f"out_rows{i}", [P, TG]) for i in range(2)]
        S = [pb(f"scores{i}", [P, TG]) for i in range(SB)]
        M = [pb(f"max_scores{i}", [P, 1024]) for i in range(2)]
        O = pb("attended", [P, TG])

        tables = sem("tables")
        ones_set = sem("ones_set")
        ident_set = sem("ident_set")
        q_loaded = [[sem(f"q_loaded{i}_{c}") for c in range(GROUPS)] for i in range(2)]
        k_loaded = [[sem(f"k_loaded{i}_{c}") for c in range(GROUPS)] for i in range(2)]
        v_loaded = [sem(f"v_loaded{i}") for i in range(2)]
        shift_loaded = [sem(f"shift_loaded{c}") for c in range(GROUPS)]
        scores_ready = sem("scores_ready")
        decayed = sem("decayed")
        exp_done = sem("exp_done")
        weighted = sem("weighted")
        pv_done = sem("pv_done")
        out_copied = sem("out_copied")
        out_stored = [sem(f"out_stored{i}") for i in range(2)]
        max_ready = sem("max_ready")
        max_read = sem("max_read")
        max_joined = sem("max_joined")
        high_ready = sem("high_ready")
        neg_ready = sem("neg_ready")
        slots_loaded = 16 * len(Q_SLOTS)

        block = ctx.enter_context(nc.Block())

        def run(eng, slot):
            for s in range(CUT):
                slot(0, 0, s)
            with eng.Fori(0, NG // 2 - 1) as turn:
                for s in range(CUT, NS):
                    slot(turn, 0, s)
                for s in range(NS):
                    slot(turn, 1, s)
                for s in range(CUT):
                    slot(turn + 1, 0, s)
            for s in range(CUT, NS):
                slot(NG // 2 - 1, 0, s)
            for s in range(NS):
                slot(NG // 2 - 1, 1, s)

        def is_last(turn, parity):
            return isinstance(turn, int) and 2 * turn + parity == NG - 1

        def reloads(turn, parity):
            return not isinstance(turn, int) or 2 * turn + parity < NG - 2

        def before(turn, parity, back):
            return (turn, parity) if not back else (turn, 0) if parity else (turn - 1, 1)

        def exists(turn, parity):
            return not isinstance(turn, int) or turn >= 0

        def count(turn, parity, each, n):
            return turn * (2 * each) + (parity * each + n)

        def wait(eng, semaphore, value):
            if not isinstance(value, int) or value > 0:
                eng.wait_ge(semaphore, value)

        def decay_operands(s, h0, h1):
            q, j = STEPS[s]
            c = first_column(s)
            x = TG * q + c - P * j
            return (W[:, s % PS, h0:h1, c:TG],
                    mul_t[:, x:x + TG - c].unsqueeze(1).to_broadcast([P, h1 - h0, TG - c]))

        def owner(turn, parity, late):
            return (turn, parity) if late else (turn, 1) if parity == 0 else (turn + 1, 0)

        @block.sync
        def _(sp):
            def load_slots(dst, src, which, loaded, c):
                rows = src.rearrange("(h d) w n -> d h w n", d=DK)[:, :, :, c * TG:(c + 1) * TG]
                for n, piece in enumerate(which):
                    sp.dma_start(dst[n * DK:(n + 1) * DK, :, :], rows[:, :, piece, :]).then_inc(loaded, 16)

            def load_q(it, parity, c):
                load_slots(QA[parity][:, c, :, :], qs[it], Q_SLOTS, q_loaded[parity][c], c)

            def load_k(it, parity, c):
                load_slots(KA[parity][:, :, c * TG:(c + 1) * TG], ks[it], K_SLOTS, k_loaded[parity][c], c)

            def load_v(it, parity):
                sp.dma_start(V[parity][:].rearrange("p t h c -> p t (h c)"),
                             vs[it]).then_inc(v_loaded[parity], 16)

            def load_shift(parity, q, read):
                sp.wait_ge(max_read, read)
                for w in range(2):
                    sp.dma_start(QA[parity][KROWS + w:KROWS + w + 1, q, :, :].rearrange("p h (r n) -> p (h r) n", n=P),
                                 mrow[w * HG * TT:(w + 1) * HG * TT, q % 2, :]).then_inc(shift_loaded[q], 16)

            def store_rows(turn, parity, q):
                sp.wait_ge(out_copied, count(turn, parity, GROUPS, q + 1))
                sp.dma_start(ao[turn * 2 + parity][:, q * TG:(q + 1) * TG], ot[q % 2][:]
                             ).then_inc(out_stored[q % 2], 16)

            def slot(turn, parity, s):
                q, j = STEPS[s]
                back, t = delayed(s, LAG)
                at = before(turn, parity, back)
                if exists(*at) and t == LAST[STEPS[t][0]]:
                    store_rows(*at, STEPS[t][0])
                    if t == NS - 1 and reloads(*at):
                        load_v(at[0] * 2 + (at[1] + 2), at[1])
                for x in range(HG * s, HG * (s + 1)):
                    what = in_ring(x, is_last(turn, parity))
                    if what and what[0] == "rows":
                        k = ring_count(x + 1, is_last(turn, parity))
                        load_shift(owner(turn, parity, what[2])[1], what[1],
                                   count(turn, parity, MAX_ITEMS, MAX_FIRST + k))
                if not reloads(turn, parity):
                    return
                done = count(turn, parity, ITEMS, HG * (s + 1))
                for g in range(GROUPS):
                    if s == max(LAST[g], CUT):
                        sp.wait_ge(scores_ready, done)
                        load_q(turn * 2 + (parity + 2), parity, g)
                if q == GROUPS - 1 and j % 4 == 3 and j < 4 * q:
                    sp.wait_ge(scores_ready, done)
                    load_k(turn * 2 + (parity + 2), parity, j // 4)
                if s == NS - 1:
                    load_k(turn * 2 + (parity + 2), parity, GROUPS - 1)

            for c in range(GROUPS):
                load_q(0, 0, c)
                load_k(0, 0, c)
                if c == 0:
                    for dst, src in ((mask_in[0], mask_kq), (mask_in[1], mask_qk), (ident, ident_in), (mul_t, tab_mul)):
                        sp.dma_start(dst[:], src).then_inc(tables, 16)
            for c in range(GROUPS):
                load_q(1, 1, c)
                load_k(1, 1, c)
            for i in range(2):
                load_v(i, i)
            m = 0
            for what, q, which in opening():
                m += what == "chunk" or which == 3
                if what == "stage" and which == 3:
                    load_shift(0, q, m)
            run(sp, slot)
            store_rows(NG // 2 - 1, 1, GROUPS - 1)
            for i in range(2):
                sp.wait_ge(out_stored[i], 16 * GROUPS * NG // 2)

        @block.tensor
        def _(pe):
            def max_scores(parity, q, chunk, m, bank):
                h, r, _, k0, width = chunk
                wait(pe, max_read, m - 1)
                for c in range(0, width, TG):
                    w = min(TG, width - c)
                    diagonal = k0 + c + w == TG * q + P * (r + 1)
                    last = nc.tensor.matmul(M[bank][:, c:c + w], QA[parity][0:KROWS, q, h, r * P:(r + 1) * P],
                                            KA[parity][0:KROWS, h, k0 + c:k0 + c + w], start=True, stop=not diagonal)
                    if diagonal:
                        last = nc.tensor.matmul(M[bank][:, c + w - P:c + w], identb[:], mask[1][:],
                                                start=False, stop=True)
                last.then_inc(max_ready, 1)

            def max_rows(q, ready, m, bank):
                pe.wait_ge(neg_ready, ready)
                wait(pe, max_read, m - 1)
                nc.tensor.transpose(M[bank][0:2 * HG * TT, 0:P // 2].bitcast(BF16),
                                    mneg[:, q % 2, :, :].rearrange("p w c -> p (w c)"), identb[:]
                                    ).then_inc(max_ready, 1)

            def pv(turn, parity, s):
                q, j = STEPS[s]
                if s == 0:
                    pe.wait_ge(v_loaded[parity], turn * 16 + 16)
                if s == FIRST[q]:
                    wait(pe, out_copied, count(turn, parity, GROUPS, q))
                if pool_heads(s):
                    pe.wait_ge(weighted, count(turn, parity, len(POOLED), POOLED.index(s) + 1))
                if pool_heads(s) < HG:
                    pe.wait_ge(decayed, count(turn, parity, len(SHARED), SHARED.index(s) + 1))
                c = first_column(s)
                for h in range(HG):
                    last = nc.tensor.matmul(O[VC * h:VC * (h + 1), c:TG], V[parity][:, j, h, :],
                                            W[:, s % PS, h, c:TG], start=(s == FIRST[q]), stop=(s == LAST[q]),
                                            tile_position=(0, VC * h))
                last.then_inc(pv_done, 1)

            def slot(turn, parity, s):
                q, j = STEPS[s]
                c = first_column(s)
                ahead = not is_last(turn, parity)
                if s == FIRST[q]:
                    pe.wait_ge(shift_loaded[q], count(turn, parity, 32, 32))
                for h in range(HG):
                    bank, reuse = score_bank(parity, HG * s + h)
                    wait(pe, exp_done, count(turn, parity, ITEMS, HG * s + h - reuse + 1))
                    last = nc.tensor.matmul(S[bank][:, c:TG], KA[parity][0:SROWS, h, j * P:(j + 1) * P],
                                            QA[parity][0:SROWS, q, h, c:TG], start=True,
                                            stop=j < 4 * q)
                    if j >= 4 * q:
                        last = nc.tensor.matmul(S[bank][:, c:c + P], identb[:], mask[0][:], start=False, stop=True)
                    last.then_inc(scores_ready, 1)
                    x = HG * s + h + ADVANCE
                    what = in_ring(x, not ahead)
                    m = MAX_FIRST + ring_count(x, not ahead)
                    if what and what[0] == "chunk":
                        _, g, chunk = what
                        if chunk == max_chunks(g)[0]:
                            loads = (turn + (1 + parity)) * slots_loaded
                            pe.wait_ge(q_loaded[1 - parity][g], loads)
                            pe.wait_ge(k_loaded[1 - parity][g], loads)
                        max_scores(1 - parity, g, chunk, count(turn, parity, MAX_ITEMS, m), m % 2)
                    elif what:
                        _, g, late = what
                        max_rows(g, count(*owner(turn, parity, late), GROUPS, g + 1),
                                 count(turn, parity, MAX_ITEMS, m), m % 2)
                back, t = delayed(s, LAG)
                at = before(turn, parity, back)
                if exists(*at):
                    pv(*at, t)

            pe.wait_ge(tables, 64)
            pe.wait_ge(ident_set, 3)
            m = 0
            for what, q, which in opening():
                if what == "chunk":
                    if which == max_chunks(q)[0]:
                        pe.wait_ge(q_loaded[0][q], slots_loaded)
                        pe.wait_ge(k_loaded[0][q], slots_loaded)
                    max_scores(0, q, which, m, m % 2)
                    m += 1
                elif which == 3:
                    max_rows(q, q + 1, m, m % 2)
                    m += 1
            pe.wait_ge(ones_set, 2)
            run(pe, slot)
            for s in range(NS - LAG, NS):
                pv(NG // 2 - 1, 1, s)

        @block.vector
        def _(dve):
            def maxima(q, chunk, m, bank):
                h, r, part, k0, width = chunk
                dve.wait_ge(max_ready, m + 1)
                nc.vector.tensor_reduce(mpart[:, q % 2, part, h * TT + r:h * TT + r + 1], M[bank][:, 0:width],
                                        mybir.AxisListType.X, ALU.max).then_inc(max_read, 1)

            def stage(q, n, turn, parity, m, bank):
                whole, other = mpart[:, q % 2, 0, :], mpart[:, q % 2, 1, :]
                high, low = mneg[:, q % 2, 0, :], mneg[:, q % 2, 1, :]
                if n == 0:
                    dve.wait_ge(max_read, m)
                    if TG * q + P > 1024:
                        nc.vector.tensor_tensor(whole, whole, other, ALU.max).then_inc(max_joined, 1)
                    else:
                        nc.vector.nop().then_inc(max_joined, 1)
                elif n == 1:
                    dve.wait_ge(max_joined, count(turn, parity, GROUPS, q + 1))
                    nc.vector.tensor_scalar_mul(high, whole, -1.0).then_inc(high_ready, 1)
                elif n == 2:
                    dve.wait_ge(high_ready, count(turn, parity, GROUPS, q + 1))
                    nc.vector.scalar_tensor_tensor(out=low, in0=whole, scalar=-1.0, in1=high,
                                                   op0=ALU.mult, op1=ALU.subtract).then_inc(neg_ready, 1)
                elif n == 3:
                    older = (q - 2, turn, parity) if q >= 2 else (q + 2, *before(turn, parity, 1))
                    wait(dve, shift_loaded[older[0]], count(older[1], older[2], 32, 32))
                    dve.wait_ge(max_ready, m + 1)
                    nc.vector.tensor_copy(mrow[:, q % 2, :], M[bank][0:2 * HG * TT, 0:P // 2].bitcast(BF16)
                                          ).then_inc(max_read, 1)

            def decay(turn, parity, s):
                heads = pool_heads(s)
                if heads < HG:
                    dve.wait_ge(exp_done, count(turn, parity, ITEMS, HG * (s + 1)))
                    w, decays = decay_operands(s, heads, HG)
                    nc.vector.tensor_tensor(w, w, decays, ALU.mult).then_inc(decayed, 1)

            def slot(turn, parity, s):
                for h in range(HG):
                    what = in_ring(HG * s + h, is_last(turn, parity))
                    m = MAX_FIRST + ring_count(HG * s + h, is_last(turn, parity))
                    if what and what[0] == "chunk":
                        maxima(*what[1:], count(turn, parity, MAX_ITEMS, m), m % 2)
                    elif what:
                        stage(what[1], 3, *owner(turn, parity, what[2]), count(turn, parity, MAX_ITEMS, m), m % 2)
                    m += what is not None
                    for g, n, late in STAGES[HG * s + h]:
                        if late or not is_last(turn, parity):
                            stage(g, n, *owner(turn, parity, late), count(turn, parity, MAX_ITEMS, m), m % 2)
                back, t = delayed(s, DECAY_LAG)
                at = before(turn, parity, back)
                if exists(*at):
                    decay(*at, t)

            dve.wait_ge(tables, 64)
            nc.vector.tensor_copy(identb[:], ident[:]).then_inc(ident_set, 1)
            for i in range(2):
                nc.vector.tensor_copy(mask[i][:], mask_in[i][:]).then_inc(ident_set, 1)
            m = 0
            for what, q, which in opening():
                if what == "chunk":
                    maxima(q, which, m, m % 2)
                else:
                    stage(q, which, 0, 0, m, m % 2)
                m += what == "chunk" or which == 3
            run(dve, slot)
            for s in range(NS - DECAY_LAG, NS):
                decay(NG // 2 - 1, 1, s)

        @block.scalar
        def _(act):
            def copy_rows(turn, parity, q):
                act.wait_ge(pv_done, count(turn, parity, NS, LAST[q] + 1))
                wait(act, out_stored[q % 2], count(turn, parity, 32, 16 * (q // 2)))
                nc.scalar.activation(ot[q % 2][:], O[:], ACT.Copy).then_inc(out_copied, 1)

            def slot(turn, parity, s):
                c = first_column(s)
                wait(act, pv_done, count(turn, parity, NS, s - PS + 1))
                for h in range(HG):
                    bank, _ = score_bank(parity, HG * s + h)
                    act.wait_ge(scores_ready, count(turn, parity, ITEMS, HG * s + h + 1))
                    nc.scalar.activation(W[:, s % PS, h, c:TG], S[bank][:, c:TG], ACT.Exp, scale=SCORE_SCALE
                                         ).then_inc(exp_done, 1)
                back, t = delayed(s, LAG)
                at = before(turn, parity, back)
                if exists(*at) and t == LAST[STEPS[t][0]]:
                    copy_rows(*at, STEPS[t][0])

            run(act, slot)
            copy_rows(NG // 2 - 1, 1, GROUPS - 1)

        @block.gpsimd
        def _(pool):
            def slot(turn, parity, s):
                heads = pool_heads(s)
                if heads:
                    pool.wait_ge(exp_done, count(turn, parity, ITEMS, HG * s + heads))
                    w, decays = decay_operands(s, 0, heads)
                    nc.gpsimd.tensor_tensor(w, w, decays, ALU.mult).then_inc(weighted, 1)

            for i in range(2):
                nc.gpsimd.memset(KA[i][KROWS:SROWS, :, :], 1.0).then_inc(ones_set, 1)
            pool.wait_ge(tables, 64)
            run(pool, slot)


def finish(nc, x, wo, bo, w_gate, w_up, w_down, ident_in, ao, rden, out):
    ctx = ExitStack()
    with ctx:
        sb = lambda n, s, d=F32: ctx.enter_context(nc.sbuf_tensor(n, s, d))
        pb = lambda n, s, d=F32: ctx.enter_context(nc.psum_tensor(n, s, d))
        sem = lambda n: ctx.enter_context(nc.semaphore(n))
        wo_sb = sb("wo_sb", [P, DC, D])
        bias_o = sb("bias_o", [P, D])
        ident = sb("ident_c", [P, P])
        sums = sb("row_sums", [P, N // 2])
        wi = [sb(f"w_int{i}", [P, HC, D], I32) for i in range(2)] + [sb("w_int2", [P, DC, HIDDEN], I32)]
        wf = [sb(f"w_float{i}", [P, HC, D]) for i in range(2)] + [sb("w_float2", [P, DC, HIDDEN])]
        wT = [sb(f"w_inT{i}", [P, DC, HIDDEN]) for i in range(2)]
        dT = sb("w_downT", [P, HC, D])
        num = [sb(f"num{i}", [P, DC, TG]) for i in range(2)]
        rd = [sb(f"rd{i}", [P, DC, TG]) for i in range(2)]
        xt = [sb(f"x_in{i}", [P, TT, D]) for i in range(2)]
        x1 = [sb(f"x_mid{i}", [P, TT, D]) for i in range(2)]
        xn = [sb(f"x_norm2_{i}", [P, TT, D]) for i in range(2)]
        xT = [sb(f"x_norm2T{i}", [P, DC, TG]) for i in range(2)]
        hT = sb("hiddenT", [P, HC, TG])
        sg = [sb(f"silu{i}", [P, TG]) for i in range(2)]
        y = [sb(f"y{i}", [P, TT, D]) for i in range(2)]
        stats = sb("stats2", [P, TT, 6])
        mv = sb("mean_var2", [P, TT, 2])
        std = sb("std2", [P, TT])
        rstd = sb("rstd2", [P, TT])
        wo_ps = [pb(f"wo_ps{i}", [P, TG]) for i in range(2)]
        dn_ps = [pb(f"dn_ps{i}", [P, TG]) for i in range(2)]
        g_ps = [pb(f"g_ps{i}", [P, TG]) for i in range(2)]
        u_ps = [pb(f"u_ps{i}", [P, TG]) for i in range(2)]

        consts = sem("consts")
        sums_in = sem("sums_in")
        inverted = sem("inverted")
        rden_out = sem("rden_out")
        cast = sem("w_cast")
        w_turned = sem("w_turned")
        w_copied = sem("w_copied")
        loaded = [sem(f"c_loaded{i}") for i in range(2)]
        biased = sem("biased")
        a_ready = sem("a_ready")
        wo_done = sem("wo_done")
        x1_ready = sem("x1_ready")
        mv_done = sem("mv_done2")
        stats_done = sem("stats_done2")
        gate = sem("gate2")
        eps_added = sem("eps_added2")
        std_ready = sem("std_ready2")
        rstd_ready = sem("rstd_ready2")
        xn_ready = sem("xn_ready2")
        transposed = sem("transposed2")
        xT_ready = sem("xT_ready2")
        gu_ready = sem("gu_ready")
        silu_ready = sem("silu_ready")
        h_ready = sem("h_ready")
        down_ready = sem("down_ready")
        y_ready = sem("y_ready")
        stored = [sem(f"stored{i}") for i in range(2)]
        block = ctx.enter_context(nc.Block())
        ao_rows = ao.rearrange("g (h r) n -> (g h) r n", r=VC)

        @block.sync
        def _(sp):
            sp.dma_start(sums[:], ao_rows[:, DK, :].rearrange("h (a n) -> h a n", a=2)).then_inc(sums_in, 16)
            for dst, src in zip(wi, (w_gate, w_up, w_down)):
                sp.dma_start(dst[:], src.rearrange("(c p) n -> p c n", p=P)).then_inc(consts, 16)
            sp.dma_start(wo_sb[:], wo.rearrange("(c p) n -> p c n", p=P)).then_inc(consts, 16)
            sp.dma_start(bias_o[:], bo.partition_broadcast(P)).then_inc(consts, 16)
            sp.dma_start(ident[:], ident_in).then_inc(consts, 16)
            sp.wait_ge(inverted, 1)
            sp.dma_start(rden.rearrange("h (a n) -> h a n", a=2), sums[:]).then_inc(rden_out, 16)
            sp.wait_ge(rden_out, 16)
            with sp.Fori(0, B) as b:
                def load(k):
                    i, cols = k % 2, slice(k * TG, (k + 1) * TG)
                    if k >= 2:
                        sp.wait_ge(x1_ready, b * (4 * GROUPS) + 4 * (k - 1))
                    for c in range(DC):
                        heads = ao_rows.rearrange("(b c h) r n -> b c h r n", b=B, c=DC)[b][c]
                        recips = rden.rearrange("(b c h) n -> b c h n", b=B, c=DC)[b][c]
                        sp.dma_start(num[i][:, c, :], heads[:, 0:DK, cols]).then_inc(loaded[i], 16)
                        sp.dma_start(rd[i][:, c, :], recips[:, cols].unsqueeze(1).to_broadcast([H // DC, DK, TG])
                                     ).then_inc(loaded[i], 16)
                    sp.dma_start(xt[i][:], x[b, cols, :].rearrange("(t p) d -> p t d", p=P)).then_inc(loaded[i], 16)
                load(0)
                for k in range(GROUPS):
                    if k + 1 < GROUPS:
                        load(k + 1)
                    sp.wait_ge(y_ready, b * (4 * GROUPS) + 4 * (k + 1))
                    sp.dma_start(out[b, k * TG:(k + 1) * TG, :].rearrange("(t p) d -> p t d", p=P), y[k % 2][:]
                                 ).then_inc(stored[k % 2], 16)
            for i in range(2):
                sp.wait_ge(stored[i], 16 * B * GROUPS // 2)

        @block.gpsimd
        def _(pool):
            pool.wait_ge(consts, 16 * 6)
            with pool.Fori(0, B) as b:
                for k in range(GROUPS):
                    i = k % 2
                    pool.wait_ge(loaded[i], b * 160 + 80 * (k // 2 + 1))
                    for t in range(TT):
                        last = nc.gpsimd.tensor_tensor(xt[i][:, t, :], xt[i][:, t, :], bias_o[:], ALU.add)
                    last.then_inc(biased, 1)

        @block.vector
        def _(dve):
            dve.wait_ge(sums_in, 16)
            nc.vector.reciprocal(sums[:], sums[:]).then_inc(inverted, 1)
            dve.wait_ge(consts, 16 * 6)
            for i in range(3):
                nc.vector.tensor_copy(wf[i][:], wi[i][:]).then_inc(cast, 1)
            with dve.Fori(0, B) as b:
                def attended(k):
                    i = k % 2
                    dve.wait_ge(loaded[i], b * 160 + 80 * (k // 2 + 1))
                    nc.vector.tensor_tensor(num[i][:], num[i][:], rd[i][:], ALU.mult).then_inc(a_ready, 1)

                def norm(k):
                    i = k % 2
                    dve.wait_ge(biased, b * GROUPS + (k + 1))
                    for t in range(TT):
                        if t % 2 == 0:
                            dve.wait_ge(wo_done, b * (2 * GROUPS) + (2 * k + t // 2 + 1))
                        nc.vector.tensor_tensor(x1[i][:, t, :], wo_ps[t // 2][:, (t % 2) * D:(t % 2 + 1) * D],
                                                xt[i][:, t, :], ALU.add).then_inc(x1_ready, 1)
                    for t in range(TT):
                        if t == 0:
                            dve.wait_ge(x1_ready, b * (4 * GROUPS) + 4 * (k + 1))
                        nc.vector.bn_stats(stats[:, t, :], x1[i][:, t, :]).then_inc(stats_done, 1)
                    dve.wait_ge(stats_done, b * (4 * GROUPS) + 4 * (k + 1))
                    nc.vector.nop().then_inc(gate, 1)
                    for t in range(TT):
                        nc.vector.bn_aggr(mv[:, t, :], stats[:, t, :]).then_inc(mv_done, 1)
                    dve.wait_ge(mv_done, b * (4 * GROUPS) + 4 * (k + 1))
                    nc.vector.tensor_scalar_add(std[:], mv[:, :, 1], EPS).then_inc(eps_added, 1)
                    dve.wait_ge(std_ready, b * GROUPS + (k + 1))
                    nc.vector.reciprocal(rstd[:], std[:]).then_inc(rstd_ready, 1)
                    dve.wait_ge(rstd_ready, b * GROUPS + (k + 1))
                    for t in range(TT):
                        last = nc.vector.tensor_scalar(xn[i][:, t, :], x1[i][:, t, :], mv[:, t, 0:1],
                                                       rstd[:, t:t + 1], ALU.subtract, ALU.mult)
                    last.then_inc(xn_ready, 1)

                attended(0)
                norm(0)
                for k in range(GROUPS):
                    if k + 1 < GROUPS:
                        attended(k + 1)
                    if k:
                        dve.wait_ge(down_ready, b * (2 * GROUPS) + 2 * k)
                    for m in range(HC):
                        dve.wait_ge(silu_ready, b * (HC * GROUPS) + (HC * k + m + 1))
                        nc.vector.scalar_tensor_tensor(out=hT[:, m, :], in0=u_ps[m % 2][:], scalar=W_SCALE,
                                                       in1=sg[m % 2][:], op0=ALU.mult, op1=ALU.mult
                                                       ).then_inc(h_ready, 1)
                    if k + 1 < GROUPS:
                        norm(k + 1)
                    if k >= 2:
                        dve.wait_ge(stored[k % 2], b * 32 + 16 * (k // 2))
                    for t in range(TT):
                        if t % 2 == 0:
                            dve.wait_ge(down_ready, b * (2 * GROUPS) + (2 * k + t // 2 + 1))
                        nc.vector.scalar_tensor_tensor(
                            out=y[k % 2][:, t, :], in0=dn_ps[t // 2][:, (t % 2) * D:(t % 2 + 1) * D],
                            scalar=W_SCALE, in1=x1[k % 2][:, t, :], op0=ALU.mult, op1=ALU.add).then_inc(y_ready, 1)
                for i in range(2):
                    dve.wait_ge(stored[i], b * 32 + 32)

        @block.scalar
        def _(act):
            n = 0
            for i in range(3):
                for c in range(DC if i < 2 else HC):
                    for part in range(2 if i < 2 else 1):
                        w = (TG, HIDDEN - TG)[part] if i < 2 else D
                        act.wait_ge(w_turned, n + 1)
                        dst = wT[i][:, c, part * TG:part * TG + w] if i < 2 else dT[:, c, :]
                        nc.scalar.activation(dst, g_ps[n % 2][:, 0:w], ACT.Copy).then_inc(w_copied, 1)
                        n += 1
            with act.Fori(0, B) as b:
                def root_and_copies(k):
                    act.wait_ge(eps_added, b * GROUPS + (k + 1))
                    nc.scalar.activation(std[:], std[:], ACT.Sqrt).then_inc(std_ready, 1)
                    act.wait_ge(transposed, b * GROUPS + (k + 1))
                    for c in range(DC):
                        nc.scalar.activation(xT[k % 2][:, c, :], dn_ps[c][:], ACT.Copy).then_inc(xT_ready, 1)
                root_and_copies(0)
                for k in range(GROUPS):
                    for m in range(HC):
                        act.wait_ge(gu_ready, b * (HC * GROUPS) + (HC * k + m + 1))
                        if k or m >= 2:
                            act.wait_ge(h_ready, b * (HC * GROUPS) + (HC * k + m - 1))
                        nc.scalar.activation(sg[m % 2][:], g_ps[m % 2][:], ACT.Silu, scale=W_SCALE
                                             ).then_inc(silu_ready, 1)
                    if k + 1 < GROUPS:
                        root_and_copies(k + 1)
                act.wait_ge(h_ready, b * (HC * GROUPS) + HC * GROUPS)

        @block.tensor
        def _(pe):
            pe.wait_ge(consts, 16 * 6)
            n = 0
            for i in range(3):
                pe.wait_ge(cast, i + 1)
                for c in range(DC if i < 2 else HC):
                    for part in range(2 if i < 2 else 1):
                        w = (TG, HIDDEN - TG)[part] if i < 2 else D
                        if n >= 2:
                            pe.wait_ge(w_copied, n - 1)
                        for a in range(w // P):
                            src = (wf[i][:, part * TT + a, c * P:(c + 1) * P] if i < 2
                                   else wf[i][:, a, c * P:(c + 1) * P])
                            last = nc.tensor.transpose(g_ps[n % 2][:, a * P:(a + 1) * P], src, ident[:])
                        last.then_inc(w_turned, 1)
                        n += 1
            pe.wait_ge(w_copied, n)
            with pe.Fori(0, B) as b:
                def out_proj(k):
                    pe.wait_ge(a_ready, b * GROUPS + (k + 1))
                    if k:
                        pe.wait_ge(x1_ready, b * (4 * GROUPS) + 4 * k)
                    for t in range(TT):
                        for c in range(DC):
                            last = nc.tensor.matmul(wo_ps[t // 2][:, (t % 2) * D:(t % 2 + 1) * D],
                                                    num[k % 2][:, c, t * P:(t + 1) * P], wo_sb[:, c, :],
                                                    start=(c == 0), stop=(c == DC - 1))
                        if t % 2:
                            last.then_inc(wo_done, 1)

                def transposes(k):
                    pe.wait_ge(xn_ready, b * GROUPS + (k + 1))
                    if k:
                        pe.wait_ge(y_ready, b * (4 * GROUPS) + 4 * k)
                    for c in range(DC):
                        for t in range(TT):
                            last = nc.tensor.transpose(dn_ps[c][:, t * P:(t + 1) * P],
                                                       xn[k % 2][:, t, c * P:(c + 1) * P], ident[:])
                    last.then_inc(transposed, 1)

                out_proj(0)
                transposes(0)
                for k in range(GROUPS):
                    pe.wait_ge(xT_ready, b * (2 * GROUPS) + 2 * (k + 1))
                    for m in range(HC):
                        if k or m >= 2:
                            pe.wait_ge(h_ready, b * (HC * GROUPS) + (HC * k + m - 1))
                        for w, ps in ((wT[0], g_ps), (wT[1], u_ps)):
                            for c in range(DC):
                                last = nc.tensor.matmul(ps[m % 2][:], w[:, c, m * P:(m + 1) * P], xT[k % 2][:, c, :],
                                                        start=(c == 0), stop=(c == DC - 1))
                        last.then_inc(gu_ready, 1)
                    if k + 1 < GROUPS:
                        out_proj(k + 1)
                    pe.wait_ge(h_ready, b * (HC * GROUPS) + HC * (k + 1))
                    for t in range(TT):
                        for m in range(HC):
                            last = nc.tensor.matmul(dn_ps[t // 2][:, (t % 2) * D:(t % 2 + 1) * D],
                                                    hT[:, m, t * P:(t + 1) * P], dT[:, m, :],
                                                    start=(m == 0), stop=(m == HC - 1))
                        if t % 2:
                            last.then_inc(down_ready, 1)
                    if k + 1 < GROUPS:
                        transposes(k + 1)
                pe.wait_ge(y_ready, b * (4 * GROUPS) + 4 * GROUPS)
                pe.wait_ge(x1_ready, b * (4 * GROUPS) + 4 * GROUPS)


def build(nc, x, wq, bq, wk, bk, wv, bv, wo, bo, w_gate, w_up, w_down, mask_kq, mask_qk, tab_mul, ident, out):
    def scratch(name, shape, dtype=F32):
        return nc.dram_tensor(name, shape, dtype, kind="Internal").ap()
    qs = scratch("q_pieces", (NG, RG, PIECES, N), BF16)
    ks = scratch("k_pieces", (NG, RG, PIECES, N), BF16)
    vs = scratch("v_ones", (NG, P, KT, HG * VC))
    ao = scratch("attn_rows", (NG, HG * VC, N))
    rden = scratch("row_reciprocals", (B * H, N))
    project(nc, x, wq, bq, wk, bk, wv, bv, ident, qs, ks, vs)
    attend(nc, mask_kq, mask_qk, tab_mul, ident, qs, ks, vs, ao)
    finish(nc, x, wo, bo, w_gate, w_up, w_down, ident, ao, rden, out)


def tables():
    key, query = np.arange(P)[:, None], np.arange(N)[None, :]
    mask = np.where(key > query[:, :P], MASKED, 0.0).astype(np.float32)
    decay = np.maximum(query - key, 1).astype(np.float64) ** -DECAY
    return mask, np.ascontiguousarray(mask.T), decay.astype(np.float32)


def kernel(**inputs):
    import concourse.bacc as bacc
    from concourse.bass_utils import run_bass_kernel_spmd

    nc = bacc.Bacc("TRN2", target_bir_lowering=False, num_devices=1)
    names = ["L0_attn_" + n for n in ("x", "Wq", "bq", "Wk", "bk", "Wv", "bv", "Wo", "bo")]
    names += ["L0_ffn_" + n for n in ("w_gate", "w_up", "w_down")]
    arrays = {n: np.ascontiguousarray(inputs[n]) for n in names}
    arrays |= dict(zip(("mask_keys_queries", "mask_queries_keys", "decay"), tables()))
    arrays["identity"] = np.eye(P, dtype=np.float32)
    args = [nc.dram_tensor(n, a.shape, mybir.dt.from_np(a.dtype), kind="ExternalInput").ap()
            for n, a in arrays.items()]
    out = nc.dram_tensor("out", (B, N, D), F32, kind="ExternalOutput").ap()
    build(nc, *args, out)
    return run_bass_kernel_spmd(nc, [arrays], core_ids=[0]).results[0]["out"]
```

```python
import math
from contextlib import ExitStack

import numpy as np

import concourse.bass as bass
from concourse import mybir

P = 128
B, N, D = 4, 2048, 256
H = 16
DK = D // H
HIDDEN = 768
EPS = 1e-5
DECAY = 0.25
W_SCALE = 1.0 / 127.0
SCORE_SCALE = 1.0 / math.sqrt(DK)
MASKED = -3.0e38

TG = 512
GROUPS = N // TG
DC = D // P
HC = HIDDEN // P
TT = TG // P
HG = 4
NG = B * H // HG
RG = HG * DK
PIECES = 3
Q_SLOTS = (0, 1, 2, 0, 1, 0)
K_SLOTS = (0, 0, 0, 1, 1, 2)
KROWS = len(Q_SLOTS) * DK
SROWS = KROWS + 2
VC = 32
KT = N // P

F32 = mybir.dt.float32
BF16 = mybir.dt.bfloat16
I32 = mybir.dt.int32
ALU = mybir.AluOpType
ACT = mybir.ActivationFunctionType

ADVANCE = 2
CUT = 17
DECAY_LAG = 1
LAG = 5
PS = 8
EAGER = 1.001
CHUNK_START = 60
POOL_HEADS = (3, 3, 3, 3, 3, 2, 3, 3, 3, 3)
POOL_LAST = (2, 1)


def key_tiles(q):
    full, diagonal = list(range(4 * q)), list(range(4 * q, 4 * q + 4))
    return [j for i in range(4) for j in full[i * q:(i + 1) * q] + [diagonal[i]]]


STEPS = [(q, j) for q in range(GROUPS) for j in key_tiles(q)]
NS = len(STEPS)
FIRST = [STEPS.index((q, key_tiles(q)[0])) for q in range(GROUPS)]
LAST = [STEPS.index((q, key_tiles(q)[-1])) for q in range(GROUPS)]


def pool_heads(s, last):
    heads = POOL_LAST if last else POOL_HEADS
    return heads[s % len(heads)]

SB = 3
ITEMS = HG * NS


def first_column(s):
    q, j = STEPS[s]
    return P * max(0, j - 4 * q)


def score_bank(parity, n):
    i = ITEMS * parity + n
    back = SB
    if i < SB:
        last = max(k for k in range(2 * ITEMS) if k % SB == i % SB)
        back = 2 * ITEMS + i - last
    return i % SB, back


def max_chunks(q):
    out = []
    for h in range(HG):
        for r in range(TT):
            width = TG * q + P * (r + 1)
            for part in range((width + 1023) // 1024):
                out.append((h, r, part, 1024 * part, min(1024, width - 1024 * part)))
    return out


def plan_maxima():
    ring, stages = [None] * ITEMS, [[] for _ in range(ITEMS)]
    chunks = [("chunk", q, chunk) for q in range(GROUPS) for chunk in max_chunks(q)]
    share = EAGER * sum(c[2][4] + CHUNK_START for c in chunks) / (HG * sum(TG - first_column(s) for s in range(NS)))
    due = 0.0
    for x in range(ADVANCE, ITEMS):
        due += share * (TG - first_column(x // HG))
        if chunks and due > 0:
            ring[x] = chunks.pop(0)
            due -= ring[x][2][4] + CHUNK_START
    assert not chunks
    for q in range(GROUPS):
        last = q == GROUPS - 1
        end = ITEMS - 1 if last else max(x for x in range(ITEMS) if ring[x] and ring[x][:2] == ("chunk", q))
        for n in range(3):
            x = end + 1 + 2 * n
            stages[x % ITEMS].append((q, n, last))
        x = end + 6 + ADVANCE
        while ring[x % ITEMS]:
            x += 1
        assert last == (x >= ITEMS)
        ring[x % ITEMS] = ("rows", q, last)
    assert not any(ring[:ADVANCE])
    return ring, stages


RING, STAGES = plan_maxima()


def in_ring(x, last):
    what = RING[x] if x < ITEMS else None
    return what if what and (not last or (what[0] == "rows" and what[2])) else None


def ring_count(x, last):
    return sum(in_ring(y, last) is not None for y in range(x))


def opening():
    for q in range(GROUPS):
        for i, chunk in enumerate(max_chunks(q)):
            yield "chunk", q, chunk
            if q and i % 2 and i // 2 < 4:
                yield "stage", q - 1, i // 2


MAX_ITEMS = sum(len(max_chunks(q)) for q in range(GROUPS)) + GROUPS
MAX_FIRST = MAX_ITEMS - 1


def delayed(s, lag):
    return (0, s - lag) if s >= lag else (1, s - lag + NS)


def batches(eng, batch):
    batch(0)
    with eng.Fori(1, B - 1) as b:
        batch(b)
    batch(B - 1)


def ahead(b, k, n):
    if k + n < GROUPS:
        return b, k + n
    return None if isinstance(b, int) and b == B - 1 else (b + 1, k + n - GROUPS)


def upto(b, k, each, n=0):
    return b * (each * GROUPS) + (each * k + n)


def wait(eng, semaphore, value):
    if not isinstance(value, int) or value > 0:
        eng.wait_ge(semaphore, value)


def project(nc, x, wq, bq, wk, bk, wv, bv, ident_in, qs, ks, vs):
    ctx = ExitStack()
    with ctx:
        sb = lambda n, s, d=F32: ctx.enter_context(nc.sbuf_tensor(n, s, d))
        pb = lambda n, s, d=F32: ctx.enter_context(nc.psum_tensor(n, s, d))
        sem = lambda n: ctx.enter_context(nc.semaphore(n))
        w_sb = [sb(f"w_{n}", [P, DC, D]) for n in "qkv"]
        bias = [sb(f"bias_{n}", [P, DC]) for n in "qk"]
        bias_v = sb("bias_v", [P, D])
        ident = sb("ident_a", [P, P])
        xt = [sb(f"x_tok{i}", [P, TT, D]) for i in range(2)]
        xn = [sb(f"x_norm{i}", [P, TT, D]) for i in range(2)]
        xT = [sb(f"x_normT{i}", [P, DC, TG]) for i in range(2)]
        stats = sb("stats", [P, TT, 6])
        mv = sb("mean_var", [P, TT, 2])
        std = sb("std", [P, TT])
        rstd = sb("rstd", [P, TT])
        piece = [[sb(f"piece{i}_{j}", [P, PIECES, TG], BF16) for j in range(4)] for i in range(2)]
        rest = [sb(f"rest{j}", [P, TG]) for j in range(4)]
        vt = [sb(f"v_tok{i}", [P, TT, H, VC]) for i in range(2)]
        tp = [pb(f"tp{c}", [P, TG]) for c in range(DC)]
        qk = [pb(f"qk{j}", [P, TG]) for j in range(4)]
        vp = [pb(f"vp{i}", [P, 2, D]) for i in range(2)]

        w_loaded = sem("w_loaded")
        ident_loaded = sem("ident_loaded_a")
        x_loaded = [sem(f"x_loaded{i}") for i in range(2)]
        ones_set = sem("ones_set")
        mv_done = sem("mv_done")
        stats_done = sem("stats_done")
        gate = sem("gate")
        std_ready = sem("std_ready")
        eps_added = sem("eps_added")
        rstd_ready = sem("rstd_ready")
        xn_ready = sem("xn_ready")
        transposed = sem("transposed")
        xT_ready = sem("xT_ready")
        qk_ready = sem("qk_ready")
        piece1 = sem("piece1")
        rest_ready = sem("rest_ready")
        piece2 = sem("piece2")
        piece3 = sem("piece3")
        v_ready = sem("v_ready")
        v_evac = sem("v_evac")
        p_stored = [sem(f"p_stored{i}") for i in range(2)]
        v_stored = [sem(f"v_stored{i}") for i in range(2)]
        block = ctx.enter_context(nc.Block())

        @block.sync
        def _(sp):
            def load(b, k):
                wait(sp, xn_ready, upto(b, k, 1, -1))
                sp.dma_start(xt[k % 2][:], x[b, k * TG:(k + 1) * TG, :].rearrange("(t p) d -> p t d", p=P)
                             ).then_inc(x_loaded[k % 2], 16)

            def batch(b):
                for k in range(GROUPS):
                    if ahead(b, k, 2):
                        load(*ahead(b, k, 2))
                    cols = slice(k * TG, (k + 1) * TG)
                    for j in range(4):
                        sp.wait_ge(piece3, upto(b, k, 4, j + 1))
                        dst = (qs, ks)[j // 2]
                        for g in range(2):
                            sp.dma_start(dst[b * 4 + (2 * (j % 2) + g)][:, :, cols],
                                         piece[k % 2][j][64 * g:64 * g + 64, :, :]).then_inc(p_stored[k % 2], 16)
                    sp.wait_ge(v_evac, upto(b, k, 4, 4))
                    for g in range(4):
                        sp.dma_start(vs[b * 4 + g][:, k * TT:(k + 1) * TT, :],
                                     vt[k % 2][:, :, 4 * g:4 * g + 4, :].rearrange("p t h c -> p t (h c)")
                                     ).then_inc(v_stored[k % 2], 16)

            load(0, 0)
            sp.dma_start(ident[:], ident_in).then_inc(ident_loaded, 16)
            load(0, 1)
            for dst, src in zip(w_sb, (wq, wk, wv)):
                sp.dma_start(dst[:], src.rearrange("(c p) n -> p c n", p=P)).then_inc(w_loaded, 16)
            for dst, src in zip(bias, (bq, bk)):
                sp.dma_start(dst[:], src.rearrange("(c p) -> p c", p=P), allow_slow_non_contiguous=True
                             ).then_inc(w_loaded, 16)
            sp.dma_start(bias_v[:], bv.partition_broadcast(P)).then_inc(w_loaded, 16)
            batches(sp, batch)
            for i in range(2):
                sp.wait_ge(p_stored[i], 16 * 8 * B * GROUPS // 2)
                sp.wait_ge(v_stored[i], 16 * 4 * B * GROUPS // 2)

        @block.vector
        def _(dve):
            for i in range(2):
                nc.vector.memset(vt[i][:, :, :, DK:VC], 0.0).then_inc(ones_set, 1)
            dve.wait_ge(ones_set, 2)
            for i in range(2):
                nc.vector.memset(vt[i][:, :, :, DK:DK + 1], 1.0)
            def norm(b, k):
                i = k % 2
                dve.wait_ge(x_loaded[i], b * 32 + 16 * (k // 2 + 1))
                for t in range(TT):
                    nc.vector.bn_stats(stats[:, t, :], xt[i][:, t, :]).then_inc(stats_done, 1)
                dve.wait_ge(stats_done, upto(b, k, 4, 4))
                nc.vector.nop().then_inc(gate, 1)
                for t in range(TT):
                    nc.vector.bn_aggr(mv[:, t, :], stats[:, t, :]).then_inc(mv_done, 1)
                dve.wait_ge(mv_done, upto(b, k, 4, 4))
                nc.vector.tensor_scalar_add(std[:], mv[:, :, 1], EPS).then_inc(eps_added, 1)
                dve.wait_ge(std_ready, upto(b, k, 1, 1))
                nc.vector.reciprocal(rstd[:], std[:]).then_inc(rstd_ready, 1)
                dve.wait_ge(rstd_ready, upto(b, k, 1, 1))
                wait(dve, transposed, upto(b, k, 1, -1))
                for t in range(TT):
                    last = nc.vector.tensor_scalar(xn[i][:, t, :], xt[i][:, t, :], mv[:, t, 0:1],
                                                   rstd[:, t:t + 1], ALU.subtract, ALU.mult)
                last.then_inc(xn_ready, 1)

            def batch(b):
                for k in range(GROUPS):
                    for j in range(4):
                        dve.wait_ge(piece1, upto(b, k, 4, j + 1))
                        wait(dve, piece3, upto(b, k, 4, j - 3))
                        nc.vector.scalar_tensor_tensor(
                            out=rest[j][:], in0=qk[j][:], scalar=bias[j // 2][:, j % 2:j % 2 + 1],
                            in1=piece[k % 2][j][:, 0, :], op0=ALU.add, op1=ALU.subtract).then_inc(rest_ready, 1)
                    if ahead(b, k, 2):
                        norm(*ahead(b, k, 2))
                    wait(dve, v_stored[k % 2], b * 128 + 64 * (k // 2))
                    for t in range(TT):
                        dve.wait_ge(v_ready, upto(b, k, 2, t // 2 + 1))
                        nc.vector.tensor_tensor(
                            vt[k % 2][:, t, :, 0:DK], vp[t // 2][:, t % 2, :].rearrange("p (h d) -> p h d", d=DK),
                            bias_v[:].rearrange("p (h d) -> p h d", d=DK), ALU.add).then_inc(v_evac, 1)

            norm(0, 0)
            norm(0, 1)
            dve.wait_ge(w_loaded, 16 * 6)
            batches(dve, batch)

        @block.scalar
        def _(act):
            def spread(b, k):
                act.wait_ge(eps_added, upto(b, k, 1, 1))
                nc.scalar.activation(std[:], std[:], ACT.Sqrt).then_inc(std_ready, 1)

            def copies(b, k):
                act.wait_ge(transposed, upto(b, k, 1, 1))
                wait(act, v_ready, upto(b, k, 2, -2))
                for c in range(DC):
                    nc.scalar.activation(xT[k % 2][:, c, :], tp[c][:], ACT.Copy).then_inc(xT_ready, 1)

            def batch(b):
                for k in range(GROUPS):
                    def second(j):
                        act.wait_ge(rest_ready, upto(b, k, 4, j + 1))
                        nc.scalar.activation(piece[k % 2][j][:, 1, :], rest[j][:], ACT.Copy).then_inc(piece2, 1)
                    wait(act, p_stored[k % 2], b * 256 + 128 * (k // 2))
                    for j in range(4):
                        act.wait_ge(qk_ready, upto(b, k, 4, j + 1))
                        nc.scalar.activation(piece[k % 2][j][:, 0, :], qk[j][:], ACT.Identity,
                                             bias=bias[j // 2][:, j % 2:j % 2 + 1]).then_inc(piece1, 1)
                        if j:
                            second(j - 1)
                    second(3)
                    if ahead(b, k, 1):
                        copies(*ahead(b, k, 1))
                    if ahead(b, k, 2):
                        spread(*ahead(b, k, 2))

            spread(0, 0)
            spread(0, 1)
            copies(0, 0)
            act.wait_ge(w_loaded, 16 * 6)
            batches(act, batch)

        @block.gpsimd
        def _(pool):
            def batch(b):
                for k in range(GROUPS):
                    for j in range(4):
                        pool.wait_ge(piece2, upto(b, k, 4, j + 1))
                        nc.gpsimd.tensor_tensor(piece[k % 2][j][:, 2, :], rest[j][:], piece[k % 2][j][:, 1, :],
                                                ALU.subtract).then_inc(piece3, 1)
            batches(pool, batch)

        @block.tensor
        def _(pe):
            pe.wait_ge(ident_loaded, 16)

            def transposes(b, k):
                pe.wait_ge(xn_ready, upto(b, k, 1, 1))
                wait(pe, xT_ready, upto(b, k, 2))
                for c in range(DC):
                    for t in range(TT):
                        last = nc.tensor.transpose(tp[c][:, t * P:(t + 1) * P],
                                                   xn[k % 2][:, t, c * P:(c + 1) * P], ident[:])
                last.then_inc(transposed, 1)

            def batch(b):
                for k in range(GROUPS):
                    pe.wait_ge(xT_ready, upto(b, k, 2, 2))
                    for j in range(4):
                        wait(pe, rest_ready, upto(b, k, 4, j - 3))
                        for c in range(DC):
                            last = nc.tensor.matmul(qk[j][:], w_sb[j // 2][:, c, (j % 2) * P:(j % 2 + 1) * P],
                                                    xT[k % 2][:, c, :], start=(c == 0), stop=(c == DC - 1))
                        last.then_inc(qk_ready, 1)
                    if ahead(b, k, 1):
                        transposes(*ahead(b, k, 1))
                    for t in range(TT):
                        if t % 2 == 0:
                            wait(pe, v_evac, upto(b, k, 4, t - 2))
                        for c in range(DC):
                            last = nc.tensor.matmul(vp[t // 2][:, t % 2, :], xT[k % 2][:, c, t * P:(t + 1) * P],
                                                    w_sb[2][:, c, :], start=(c == 0), stop=(c == DC - 1))
                        if t % 2:
                            last.then_inc(v_ready, 1)

            transposes(0, 0)
            pe.wait_ge(w_loaded, 16 * 6)
            batches(pe, batch)


def attend(nc, mask_kq, mask_qk, tab_mul, ident_in, qs, ks, vs, ao):
    ctx = ExitStack()
    with ctx:
        sb = lambda n, s, d=F32: ctx.enter_context(nc.sbuf_tensor(n, s, d))
        pb = lambda n, s, d=F32: ctx.enter_context(nc.psum_tensor(n, s, d))
        sem = lambda n: ctx.enter_context(nc.semaphore(n))
        QA = [sb(f"q_slots{i}", [P, GROUPS, HG, TG], BF16) for i in range(2)]
        KA = [sb(f"k_slots{i}", [P, HG, N], BF16) for i in range(2)]
        V = [sb(f"v_heads{i}", [P, KT, HG, VC]) for i in range(2)]
        mul_t = sb("decay_mul", [P, N])
        ident = sb("ident_b", [P, P])
        identb = sb("ident_bf", [P, P], BF16)
        mask_in = [sb(f"mask_f{i}", [P, P]) for i in range(2)]
        mask = [sb(f"mask_bf{i}", [P, P], BF16) for i in range(2)]
        W = sb("weights", [P, PS, HG, TG])
        mpart = sb("max_parts", [P, 2, 2, HG * TT])
        mneg = sb("neg_max", [P, 2, 2, HG * TT], BF16)
        mrow = sb("max_rows", [2 * HG * TT, 2, P], BF16)
        ot = [sb(f"out_rows{i}", [P, TG]) for i in range(2)]
        S = [pb(f"scores{i}", [P, TG]) for i in range(SB)]
        M = [pb(f"max_scores{i}", [P, 1024]) for i in range(2)]
        O = pb("attended", [P, TG])

        tables = sem("tables")
        decay_loaded = sem("decay_loaded")
        ones_set = sem("ones_set")
        ident_set = sem("ident_set")
        q_loaded = [[sem(f"q_loaded{i}_{c}") for c in range(GROUPS)] for i in range(2)]
        k_loaded = [[sem(f"k_loaded{i}_{c}") for c in range(GROUPS)] for i in range(2)]
        v_loaded = [sem(f"v_loaded{i}") for i in range(2)]
        shift_loaded = [sem(f"shift_loaded{c}") for c in range(GROUPS)]
        scores_ready = sem("scores_ready")
        decayed = sem("decayed")
        exp_done = sem("exp_done")
        weighted = sem("weighted")
        pv_done = sem("pv_done")
        out_copied = sem("out_copied")
        out_stored = [sem(f"out_stored{i}") for i in range(2)]
        max_ready = sem("max_ready")
        max_read = sem("max_read")
        max_joined = sem("max_joined")
        high_ready = sem("high_ready")
        neg_ready = sem("neg_ready")
        slots_loaded = 16 * len(Q_SLOTS)

        block = ctx.enter_context(nc.Block())

        def run(eng, slot):
            for s in range(CUT):
                slot(0, 0, s)
            with eng.Fori(0, NG // 2 - 1) as turn:
                for s in range(CUT, NS):
                    slot(turn, 0, s)
                for s in range(NS):
                    slot(turn, 1, s)
                for s in range(CUT):
                    slot(turn + 1, 0, s)
            for s in range(CUT, NS):
                slot(NG // 2 - 1, 0, s)
            for s in range(NS):
                slot(NG // 2 - 1, 1, s)

        def is_last(turn, parity):
            return isinstance(turn, int) and 2 * turn + parity == NG - 1

        def reloads(turn, parity):
            return not isinstance(turn, int) or 2 * turn + parity < NG - 2

        def before(turn, parity, back):
            return (turn, parity) if not back else (turn, 0) if parity else (turn - 1, 1)

        def exists(turn, parity):
            return not isinstance(turn, int) or turn >= 0

        def count(turn, parity, each, n):
            return turn * (2 * each) + (parity * each + n)

        def decay_operands(s, h0, h1):
            q, j = STEPS[s]
            c = first_column(s)
            x = TG * q + c - P * j
            return (W[:, s % PS, h0:h1, c:TG],
                    mul_t[:, x:x + TG - c].unsqueeze(1).to_broadcast([P, h1 - h0, TG - c]))

        def owner(turn, parity, late):
            return (turn, parity) if late else (turn, 1) if parity == 0 else (turn + 1, 0)

        @block.sync
        def _(sp):
            def load_slots(dst, src, which, loaded, c):
                rows = src.rearrange("(h d) w n -> d h w n", d=DK)[:, :, :, c * TG:(c + 1) * TG]
                for n, piece in enumerate(which):
                    sp.dma_start(dst[n * DK:(n + 1) * DK, :, :], rows[:, :, piece, :]).then_inc(loaded, 16)

            def load_q(it, parity, c):
                load_slots(QA[parity][:, c, :, :], qs[it], Q_SLOTS, q_loaded[parity][c], c)

            def load_k(it, parity, c):
                load_slots(KA[parity][:, :, c * TG:(c + 1) * TG], ks[it], K_SLOTS, k_loaded[parity][c], c)

            def load_v(it, parity):
                sp.dma_start(V[parity][:].rearrange("p t h c -> p t (h c)"),
                             vs[it]).then_inc(v_loaded[parity], 16)

            def load_shift(parity, q, read):
                sp.wait_ge(max_read, read)
                for w in range(2):
                    sp.dma_start(QA[parity][KROWS + w:KROWS + w + 1, q, :, :].rearrange("p h (r n) -> p (h r) n", n=P),
                                 mrow[w * HG * TT:(w + 1) * HG * TT, q % 2, :]).then_inc(shift_loaded[q], 16)

            def store_rows(turn, parity, q):
                sp.wait_ge(out_copied, count(turn, parity, GROUPS, q + 1))
                sp.dma_start(ao[turn * 2 + parity][:, q * TG:(q + 1) * TG], ot[q % 2][:]
                             ).then_inc(out_stored[q % 2], 16)

            def slot(turn, parity, s):
                q, j = STEPS[s]
                back, t = delayed(s, LAG)
                at = before(turn, parity, back)
                if exists(*at) and t == LAST[STEPS[t][0]]:
                    store_rows(*at, STEPS[t][0])
                    if t == NS - 1 and reloads(*at):
                        load_v(at[0] * 2 + (at[1] + 2), at[1])
                for x in range(HG * s, HG * (s + 1)):
                    what = in_ring(x, is_last(turn, parity))
                    if what and what[0] == "rows":
                        k = ring_count(x + 1, is_last(turn, parity))
                        load_shift(owner(turn, parity, what[2])[1], what[1],
                                   count(turn, parity, MAX_ITEMS, MAX_FIRST + k))
                if not reloads(turn, parity):
                    return
                done = count(turn, parity, ITEMS, HG * (s + 1))
                for g in range(GROUPS):
                    if s == max(LAST[g], CUT):
                        sp.wait_ge(scores_ready, done)
                        load_q(turn * 2 + (parity + 2), parity, g)
                if q == GROUPS - 1 and j % 4 == 3 and j < 4 * q:
                    sp.wait_ge(scores_ready, done)
                    load_k(turn * 2 + (parity + 2), parity, j // 4)
                if s == NS - 1:
                    load_k(turn * 2 + (parity + 2), parity, GROUPS - 1)

            for dst, src in ((mask_in[0], mask_kq), (mask_in[1], mask_qk), (ident, ident_in)):
                sp.dma_start(dst[:], src).then_inc(tables, 16)
            for c in range(GROUPS):
                load_q(0, 0, c)
                load_k(0, 0, c)
            sp.dma_start(mul_t[:], tab_mul).then_inc(decay_loaded, 16)
            for c in range(GROUPS):
                load_q(1, 1, c)
                load_k(1, 1, c)
            for i in range(2):
                load_v(i, i)
            m = 0
            for what, q, which in opening():
                m += what == "chunk" or which == 3
                if what == "stage" and which == 3:
                    load_shift(0, q, m)
            run(sp, slot)
            store_rows(NG // 2 - 1, 1, GROUPS - 1)
            for i in range(2):
                sp.wait_ge(out_stored[i], 16 * GROUPS * NG // 2)

        @block.tensor
        def _(pe):
            def max_scores(parity, q, chunk, m, bank):
                h, r, _, k0, width = chunk
                wait(pe, max_read, m - 1)
                for c in range(0, width, TG):
                    w = min(TG, width - c)
                    diagonal = k0 + c + w == TG * q + P * (r + 1)
                    last = nc.tensor.matmul(M[bank][:, c:c + w], QA[parity][0:KROWS, q, h, r * P:(r + 1) * P],
                                            KA[parity][0:KROWS, h, k0 + c:k0 + c + w], start=True, stop=not diagonal)
                    if diagonal:
                        last = nc.tensor.matmul(M[bank][:, c + w - P:c + w], identb[:], mask[1][:],
                                                start=False, stop=True)
                last.then_inc(max_ready, 1)

            def max_rows(q, ready, m, bank):
                pe.wait_ge(neg_ready, ready)
                wait(pe, max_read, m - 1)
                nc.tensor.transpose(M[bank][0:2 * HG * TT, 0:P // 2].bitcast(BF16),
                                    mneg[:, q % 2, :, :].rearrange("p w c -> p (w c)"), identb[:]
                                    ).then_inc(max_ready, 1)

            def pv(turn, parity, s):
                q, j = STEPS[s]
                if s == 0:
                    pe.wait_ge(v_loaded[parity], turn * 16 + 16)
                if s == FIRST[q]:
                    wait(pe, out_copied, count(turn, parity, GROUPS, q))
                pe.wait_ge(weighted, count(turn, parity, NS, s + 1))
                pe.wait_ge(decayed, count(turn, parity, NS, s + 1))
                c = first_column(s)
                for h in range(HG):
                    last = nc.tensor.matmul(O[VC * h:VC * (h + 1), c:TG], V[parity][:, j, h, :],
                                            W[:, s % PS, h, c:TG], start=(s == FIRST[q]), stop=(s == LAST[q]),
                                            tile_position=(0, VC * h))
                last.then_inc(pv_done, 1)

            def slot(turn, parity, s):
                q, j = STEPS[s]
                c = first_column(s)
                ahead = not is_last(turn, parity)
                if s == FIRST[q]:
                    pe.wait_ge(shift_loaded[q], count(turn, parity, 32, 32))
                for h in range(HG):
                    bank, reuse = score_bank(parity, HG * s + h)
                    wait(pe, exp_done, count(turn, parity, ITEMS, HG * s + h - reuse + 1))
                    last = nc.tensor.matmul(S[bank][:, c:TG], KA[parity][0:SROWS, h, j * P:(j + 1) * P],
                                            QA[parity][0:SROWS, q, h, c:TG], start=True,
                                            stop=j < 4 * q)
                    if j >= 4 * q:
                        last = nc.tensor.matmul(S[bank][:, c:c + P], identb[:], mask[0][:], start=False, stop=True)
                    last.then_inc(scores_ready, 1)
                    x = HG * s + h + ADVANCE
                    what = in_ring(x, not ahead)
                    m = MAX_FIRST + ring_count(x, not ahead)
                    if what and what[0] == "chunk":
                        _, g, chunk = what
                        if chunk == max_chunks(g)[0]:
                            loads = (turn + (1 + parity)) * slots_loaded
                            pe.wait_ge(q_loaded[1 - parity][g], loads)
                            pe.wait_ge(k_loaded[1 - parity][g], loads)
                        max_scores(1 - parity, g, chunk, count(turn, parity, MAX_ITEMS, m), m % 2)
                    elif what:
                        _, g, late = what
                        max_rows(g, count(*owner(turn, parity, late), GROUPS, g + 1),
                                 count(turn, parity, MAX_ITEMS, m), m % 2)
                back, t = delayed(s, LAG)
                at = before(turn, parity, back)
                if exists(*at):
                    pv(*at, t)

            pe.wait_ge(ident_set, 3)
            m = 0
            for what, q, which in opening():
                if what == "chunk":
                    if which == max_chunks(q)[0]:
                        pe.wait_ge(q_loaded[0][q], slots_loaded)
                        pe.wait_ge(k_loaded[0][q], slots_loaded)
                    max_scores(0, q, which, m, m % 2)
                    m += 1
                elif which == 3:
                    max_rows(q, q + 1, m, m % 2)
                    m += 1
            pe.wait_ge(ones_set, 2)
            run(pe, slot)
            for s in range(NS - LAG, NS):
                pv(NG // 2 - 1, 1, s)

        @block.vector
        def _(dve):
            def maxima(q, chunk, m, bank):
                h, r, part, k0, width = chunk
                dve.wait_ge(max_ready, m + 1)
                nc.vector.tensor_reduce(mpart[:, q % 2, part, h * TT + r:h * TT + r + 1], M[bank][:, 0:width],
                                        mybir.AxisListType.X, ALU.max).then_inc(max_read, 1)

            def stage(q, n, turn, parity, m, bank):
                whole, other = mpart[:, q % 2, 0, :], mpart[:, q % 2, 1, :]
                high, low = mneg[:, q % 2, 0, :], mneg[:, q % 2, 1, :]
                if n == 0:
                    dve.wait_ge(max_read, m)
                    if TG * q + P > 1024:
                        nc.vector.tensor_tensor(whole, whole, other, ALU.max).then_inc(max_joined, 1)
                    else:
                        nc.vector.nop().then_inc(max_joined, 1)
                elif n == 1:
                    dve.wait_ge(max_joined, count(turn, parity, GROUPS, q + 1))
                    nc.vector.tensor_scalar_mul(high, whole, -1.0).then_inc(high_ready, 1)
                elif n == 2:
                    dve.wait_ge(high_ready, count(turn, parity, GROUPS, q + 1))
                    nc.vector.scalar_tensor_tensor(out=low, in0=whole, scalar=-1.0, in1=high,
                                                   op0=ALU.mult, op1=ALU.subtract).then_inc(neg_ready, 1)
                elif n == 3:
                    older = (q - 2, turn, parity) if q >= 2 else (q + 2, *before(turn, parity, 1))
                    wait(dve, shift_loaded[older[0]], count(older[1], older[2], 32, 32))
                    dve.wait_ge(max_ready, m + 1)
                    nc.vector.tensor_copy(mrow[:, q % 2, :], M[bank][0:2 * HG * TT, 0:P // 2].bitcast(BF16)
                                          ).then_inc(max_read, 1)

            def decay(turn, parity, s):
                dve.wait_ge(exp_done, count(turn, parity, ITEMS, HG * (s + 1)))
                w, decays = decay_operands(s, pool_heads(s, is_last(turn, parity)), HG)
                nc.vector.tensor_tensor(w, w, decays, ALU.mult).then_inc(decayed, 1)

            def slot(turn, parity, s):
                for h in range(HG):
                    what = in_ring(HG * s + h, is_last(turn, parity))
                    m = MAX_FIRST + ring_count(HG * s + h, is_last(turn, parity))
                    if what and what[0] == "chunk":
                        maxima(*what[1:], count(turn, parity, MAX_ITEMS, m), m % 2)
                    elif what:
                        stage(what[1], 3, *owner(turn, parity, what[2]), count(turn, parity, MAX_ITEMS, m), m % 2)
                    m += what is not None
                    for g, n, late in STAGES[HG * s + h]:
                        if late or not is_last(turn, parity):
                            stage(g, n, *owner(turn, parity, late), count(turn, parity, MAX_ITEMS, m), m % 2)
                back, t = delayed(s, DECAY_LAG)
                at = before(turn, parity, back)
                if exists(*at):
                    decay(*at, t)

            dve.wait_ge(tables, 48)
            nc.vector.tensor_copy(identb[:], ident[:]).then_inc(ident_set, 1)
            for i in range(2):
                nc.vector.tensor_copy(mask[i][:], mask_in[i][:]).then_inc(ident_set, 1)
            m = 0
            for what, q, which in opening():
                if what == "chunk":
                    maxima(q, which, m, m % 2)
                else:
                    stage(q, which, 0, 0, m, m % 2)
                m += what == "chunk" or which == 3
            dve.wait_ge(decay_loaded, 16)
            run(dve, slot)
            for s in range(NS - DECAY_LAG, NS):
                decay(NG // 2 - 1, 1, s)

        @block.scalar
        def _(act):
            def copy_rows(turn, parity, q):
                act.wait_ge(pv_done, count(turn, parity, NS, LAST[q] + 1))
                wait(act, out_stored[q % 2], count(turn, parity, 32, 16 * (q // 2)))
                nc.scalar.activation(ot[q % 2][:], O[:], ACT.Copy).then_inc(out_copied, 1)

            def slot(turn, parity, s):
                c = first_column(s)
                wait(act, pv_done, count(turn, parity, NS, s - PS + 1))
                for h in range(HG):
                    bank, _ = score_bank(parity, HG * s + h)
                    act.wait_ge(scores_ready, count(turn, parity, ITEMS, HG * s + h + 1))
                    nc.scalar.activation(W[:, s % PS, h, c:TG], S[bank][:, c:TG], ACT.Exp, scale=SCORE_SCALE
                                         ).then_inc(exp_done, 1)
                back, t = delayed(s, LAG)
                at = before(turn, parity, back)
                if exists(*at) and t == LAST[STEPS[t][0]]:
                    copy_rows(*at, STEPS[t][0])

            run(act, slot)
            copy_rows(NG // 2 - 1, 1, GROUPS - 1)

        @block.gpsimd
        def _(pool):
            def slot(turn, parity, s):
                heads = pool_heads(s, is_last(turn, parity))
                pool.wait_ge(exp_done, count(turn, parity, ITEMS, HG * s + heads))
                w, decays = decay_operands(s, 0, heads)
                nc.gpsimd.tensor_tensor(w, w, decays, ALU.mult).then_inc(weighted, 1)

            for i in range(2):
                nc.gpsimd.memset(KA[i][KROWS:SROWS, :, :], 1.0).then_inc(ones_set, 1)
            pool.wait_ge(decay_loaded, 16)
            run(pool, slot)


def finish(nc, x, wo, bo, w_gate, w_up, w_down, ident_in, ao, rden, out):
    ctx = ExitStack()
    with ctx:
        sb = lambda n, s, d=F32: ctx.enter_context(nc.sbuf_tensor(n, s, d))
        pb = lambda n, s, d=F32: ctx.enter_context(nc.psum_tensor(n, s, d))
        sem = lambda n: ctx.enter_context(nc.semaphore(n))
        wo_sb = sb("wo_sb", [P, DC, D])
        bias_o = sb("bias_o", [P, D])
        ident = sb("ident_c", [P, P])
        sums = sb("row_sums", [P, N // 2])
        wi = [sb(f"w_int{i}", [P, HC, D], I32) for i in range(2)] + [sb("w_int2", [P, DC, HIDDEN], I32)]
        wf = [sb(f"w_float{i}", [P, HC, D]) for i in range(2)] + [sb("w_float2", [P, DC, HIDDEN])]
        wT = [sb(f"w_inT{i}", [P, DC, HIDDEN]) for i in range(2)]
        dT = sb("w_downT", [P, HC, D])
        num = [sb(f"num{i}", [P, DC, TG]) for i in range(2)]
        rd = [sb(f"rd{i}", [P, DC, TG]) for i in range(2)]
        xt = [sb(f"x_in{i}", [P, TT, D]) for i in range(2)]
        x1 = [sb(f"x_mid{i}", [P, TT, D]) for i in range(2)]
        xn = [sb(f"x_norm2_{i}", [P, TT, D]) for i in range(2)]
        xT = [sb(f"x_norm2T{i}", [P, DC, TG]) for i in range(2)]
        hT = sb("hiddenT", [P, HC, TG])
        sg = [sb(f"silu{i}", [P, TG]) for i in range(2)]
        y = [sb(f"y{i}", [P, TT, D]) for i in range(2)]
        stats = sb("stats2", [P, TT, 6])
        mv = sb("mean_var2", [P, TT, 2])
        std = sb("std2", [P, TT])
        rstd = sb("rstd2", [P, TT])
        wo_ps = [pb(f"wo_ps{i}", [P, TG]) for i in range(2)]
        dn_ps = [pb(f"dn_ps{i}", [P, TG]) for i in range(2)]
        g_ps = [pb(f"g_ps{i}", [P, TG]) for i in range(2)]
        u_ps = [pb(f"u_ps{i}", [P, TG]) for i in range(2)]

        consts = sem("consts")
        ident_in_sb = sem("ident_loaded")
        w_loaded = [sem(f"w_loaded2_{i}") for i in range(3)]
        sums_in = sem("sums_in")
        inverted = sem("inverted")
        rden_out = sem("rden_out")
        cast = sem("w_cast")
        w_turned = sem("w_turned")
        w_copied = sem("w_copied")
        loaded = [sem(f"c_loaded{i}") for i in range(2)]
        biased = sem("biased")
        a_ready = sem("a_ready")
        wo_done = sem("wo_done")
        x1_ready = sem("x1_ready")
        mv_done = sem("mv_done2")
        stats_done = sem("stats_done2")
        gate = sem("gate2")
        eps_added = sem("eps_added2")
        std_ready = sem("std_ready2")
        rstd_ready = sem("rstd_ready2")
        xn_ready = sem("xn_ready2")
        transposed = sem("transposed2")
        xT_ready = sem("xT_ready2")
        gu_ready = sem("gu_ready")
        silu_ready = sem("silu_ready")
        h_ready = sem("h_ready")
        down_ready = sem("down_ready")
        y_ready = sem("y_ready")
        stored = [sem(f"stored{i}") for i in range(2)]
        block = ctx.enter_context(nc.Block())
        ao_rows = ao.rearrange("g (h r) n -> (g h) r n", r=VC)

        @block.sync
        def _(sp):
            sp.dma_start(ident[:], ident_in).then_inc(ident_in_sb, 16)
            for i, (dst, src) in enumerate(zip(wi, (w_gate, w_up, w_down))):
                sp.dma_start(dst[:], src.rearrange("(c p) n -> p c n", p=P)).then_inc(w_loaded[i], 16)
                if i == 0:
                    sp.dma_start(sums[:], ao_rows[:, DK, :].rearrange("h (a n) -> h a n", a=2)).then_inc(sums_in, 16)
            sp.dma_start(wo_sb[:], wo.rearrange("(c p) n -> p c n", p=P)).then_inc(consts, 16)
            sp.dma_start(bias_o[:], bo.partition_broadcast(P)).then_inc(consts, 16)
            sp.wait_ge(inverted, 1)
            sp.dma_start(rden.rearrange("h (a n) -> h a n", a=2), sums[:]).then_inc(rden_out, 16)
            sp.wait_ge(rden_out, 16)

            def load(b, k):
                i, cols = k % 2, slice(k * TG, (k + 1) * TG)
                wait(sp, x1_ready, upto(b, k, 4, -4))
                for c in range(DC):
                    heads = ao_rows.rearrange("(b c h) r n -> b c h r n", b=B, c=DC)[b][c]
                    recips = rden.rearrange("(b c h) n -> b c h n", b=B, c=DC)[b][c]
                    sp.dma_start(num[i][:, c, :], heads[:, 0:DK, cols]).then_inc(loaded[i], 16)
                    sp.dma_start(rd[i][:, c, :], recips[:, cols].unsqueeze(1).to_broadcast([H // DC, DK, TG])
                                 ).then_inc(loaded[i], 16)
                sp.dma_start(xt[i][:], x[b, cols, :].rearrange("(t p) d -> p t d", p=P)).then_inc(loaded[i], 16)

            def batch(b):
                for k in range(GROUPS):
                    if ahead(b, k, 1):
                        load(*ahead(b, k, 1))
                    sp.wait_ge(y_ready, upto(b, k, 4, 4))
                    sp.dma_start(out.rearrange("b (g t p) d -> (b g) p t d", p=P, t=TT)[upto(b, k, 1)], y[k % 2][:]
                                 ).then_inc(stored[k % 2], 16)

            load(0, 0)
            batches(sp, batch)
            for i in range(2):
                sp.wait_ge(stored[i], 16 * B * GROUPS // 2)

        @block.gpsimd
        def _(pool):
            pool.wait_ge(consts, 16 * 2)

            def batch(b):
                for k in range(GROUPS):
                    i = k % 2
                    pool.wait_ge(loaded[i], b * 160 + 80 * (k // 2 + 1))
                    for t in range(TT):
                        last = nc.gpsimd.tensor_tensor(xt[i][:, t, :], xt[i][:, t, :], bias_o[:], ALU.add)
                    last.then_inc(biased, 1)
            batches(pool, batch)

        @block.vector
        def _(dve):
            for i in range(3):
                dve.wait_ge(w_loaded[i], 16)
                nc.vector.tensor_copy(wf[i][:], wi[i][:]).then_inc(cast, 1)
                if i == 0:
                    dve.wait_ge(sums_in, 16)
                    nc.vector.reciprocal(sums[:], sums[:]).then_inc(inverted, 1)

            def attended(b, k):
                i = k % 2
                dve.wait_ge(loaded[i], b * 160 + 80 * (k // 2 + 1))
                nc.vector.tensor_tensor(num[i][:], num[i][:], rd[i][:], ALU.mult).then_inc(a_ready, 1)

            def norm(b, k):
                i = k % 2
                dve.wait_ge(biased, upto(b, k, 1, 1))
                for t in range(TT):
                    if t % 2 == 0:
                        dve.wait_ge(wo_done, upto(b, k, 2, t // 2 + 1))
                    nc.vector.tensor_tensor(x1[i][:, t, :], wo_ps[t // 2][:, (t % 2) * D:(t % 2 + 1) * D],
                                            xt[i][:, t, :], ALU.add).then_inc(x1_ready, 1)
                dve.wait_ge(x1_ready, upto(b, k, 4, 4))
                for t in range(TT):
                    nc.vector.bn_stats(stats[:, t, :], x1[i][:, t, :]).then_inc(stats_done, 1)
                dve.wait_ge(stats_done, upto(b, k, 4, 4))
                nc.vector.nop().then_inc(gate, 1)
                for t in range(TT):
                    nc.vector.bn_aggr(mv[:, t, :], stats[:, t, :]).then_inc(mv_done, 1)
                dve.wait_ge(mv_done, upto(b, k, 4, 4))
                nc.vector.tensor_scalar_add(std[:], mv[:, :, 1], EPS).then_inc(eps_added, 1)
                dve.wait_ge(std_ready, upto(b, k, 1, 1))
                nc.vector.reciprocal(rstd[:], std[:]).then_inc(rstd_ready, 1)
                dve.wait_ge(rstd_ready, upto(b, k, 1, 1))
                for t in range(TT):
                    last = nc.vector.tensor_scalar(xn[i][:, t, :], x1[i][:, t, :], mv[:, t, 0:1],
                                                   rstd[:, t:t + 1], ALU.subtract, ALU.mult)
                last.then_inc(xn_ready, 1)

            def batch(b):
                for k in range(GROUPS):
                    following = ahead(b, k, 1)
                    wait(dve, down_ready, upto(b, k, 2))
                    for m in range(HC):
                        dve.wait_ge(silu_ready, upto(b, k, HC, m + 1))
                        nc.vector.scalar_tensor_tensor(out=hT[:, m, :], in0=u_ps[m % 2][:], scalar=W_SCALE,
                                                       in1=sg[m % 2][:], op0=ALU.mult, op1=ALU.mult
                                                       ).then_inc(h_ready, 1)
                        if m == HC // 2 and following:
                            attended(*following)
                    if following:
                        norm(*following)
                    wait(dve, stored[k % 2], b * 32 + 16 * (k // 2))
                    for t in range(TT):
                        if t % 2 == 0:
                            dve.wait_ge(down_ready, upto(b, k, 2, t // 2 + 1))
                        nc.vector.scalar_tensor_tensor(
                            out=y[k % 2][:, t, :], in0=dn_ps[t // 2][:, (t % 2) * D:(t % 2 + 1) * D],
                            scalar=W_SCALE, in1=x1[k % 2][:, t, :], op0=ALU.mult, op1=ALU.add).then_inc(y_ready, 1)

            attended(0, 0)
            norm(0, 0)
            batches(dve, batch)

        @block.scalar
        def _(act):
            n = 0
            for i in range(3):
                for c in range(DC if i < 2 else HC):
                    for part in range(2 if i < 2 else 1):
                        w = (TG, HIDDEN - TG)[part] if i < 2 else D
                        act.wait_ge(w_turned, n + 1)
                        dst = wT[i][:, c, part * TG:part * TG + w] if i < 2 else dT[:, c, :]
                        nc.scalar.activation(dst, g_ps[n % 2][:, 0:w], ACT.Copy).then_inc(w_copied, 1)
                        n += 1

            def root_and_copies(b, k):
                act.wait_ge(eps_added, upto(b, k, 1, 1))
                nc.scalar.activation(std[:], std[:], ACT.Sqrt).then_inc(std_ready, 1)
                act.wait_ge(transposed, upto(b, k, 1, 1))
                for c in range(DC):
                    nc.scalar.activation(xT[k % 2][:, c, :], wo_ps[c][:], ACT.Copy).then_inc(xT_ready, 1)

            def batch(b):
                for k in range(GROUPS):
                    for m in range(HC):
                        act.wait_ge(gu_ready, upto(b, k, HC, m + 1))
                        wait(act, h_ready, upto(b, k, HC, m - 1))
                        nc.scalar.activation(sg[m % 2][:], g_ps[m % 2][:], ACT.Silu, scale=W_SCALE
                                             ).then_inc(silu_ready, 1)
                    if ahead(b, k, 1):
                        root_and_copies(*ahead(b, k, 1))

            root_and_copies(0, 0)
            batches(act, batch)

        @block.tensor
        def _(pe):
            pe.wait_ge(ident_in_sb, 16)
            n = 0
            for i in range(3):
                pe.wait_ge(cast, i + 1)
                for c in range(DC if i < 2 else HC):
                    for part in range(2 if i < 2 else 1):
                        w = (TG, HIDDEN - TG)[part] if i < 2 else D
                        if n >= 2:
                            pe.wait_ge(w_copied, n - 1)
                        for a in range(w // P):
                            src = (wf[i][:, part * TT + a, c * P:(c + 1) * P] if i < 2
                                   else wf[i][:, a, c * P:(c + 1) * P])
                            last = nc.tensor.transpose(g_ps[n % 2][:, a * P:(a + 1) * P], src, ident[:])
                        last.then_inc(w_turned, 1)
                        n += 1
            pe.wait_ge(w_copied, n)

            def out_proj(b, k):
                pe.wait_ge(a_ready, upto(b, k, 1, 1))
                wait(pe, xT_ready, upto(b, k, 2))
                for t in range(TT):
                    for c in range(DC):
                        last = nc.tensor.matmul(wo_ps[t // 2][:, (t % 2) * D:(t % 2 + 1) * D],
                                                num[k % 2][:, c, t * P:(t + 1) * P], wo_sb[:, c, :],
                                                start=(c == 0), stop=(c == DC - 1))
                    if t % 2:
                        last.then_inc(wo_done, 1)

            def transposes(b, k):
                pe.wait_ge(xn_ready, upto(b, k, 1, 1))
                for c in range(DC):
                    for t in range(TT):
                        last = nc.tensor.transpose(wo_ps[c][:, t * P:(t + 1) * P],
                                                   xn[k % 2][:, t, c * P:(c + 1) * P], ident[:])
                last.then_inc(transposed, 1)

            def batch(b):
                for k in range(GROUPS):
                    following = ahead(b, k, 1)
                    pe.wait_ge(xT_ready, upto(b, k, 2, 2))
                    for m in range(HC):
                        wait(pe, h_ready, upto(b, k, HC, m - 1))
                        for w, ps in ((wT[0], g_ps), (wT[1], u_ps)):
                            for c in range(DC):
                                last = nc.tensor.matmul(ps[m % 2][:], w[:, c, m * P:(m + 1) * P], xT[k % 2][:, c, :],
                                                        start=(c == 0), stop=(c == DC - 1))
                        last.then_inc(gu_ready, 1)
                    if following:
                        out_proj(*following)
                    pe.wait_ge(h_ready, upto(b, k, HC, HC))
                    for t in range(TT):
                        if t == TT - 1 and following:
                            transposes(*following)
                        if t % 2 == 0:
                            wait(pe, y_ready, upto(b, k, 4, t - 2))
                        for m in range(HC):
                            last = nc.tensor.matmul(dn_ps[t // 2][:, (t % 2) * D:(t % 2 + 1) * D],
                                                    hT[:, m, t * P:(t + 1) * P], dT[:, m, :],
                                                    start=(m == 0), stop=(m == HC - 1))
                        if t % 2:
                            last.then_inc(down_ready, 1)

            pe.wait_ge(consts, 16 * 2)
            out_proj(0, 0)
            transposes(0, 0)
            batches(pe, batch)


def build(nc, x, wq, bq, wk, bk, wv, bv, wo, bo, w_gate, w_up, w_down, mask_kq, mask_qk, tab_mul, ident, out):
    def scratch(name, shape, dtype=F32):
        return nc.dram_tensor(name, shape, dtype, kind="Internal").ap()
    qs = scratch("q_pieces", (NG, RG, PIECES, N), BF16)
    ks = scratch("k_pieces", (NG, RG, PIECES, N), BF16)
    vs = scratch("v_ones", (NG, P, KT, HG * VC))
    ao = scratch("attn_rows", (NG, HG * VC, N))
    rden = scratch("row_reciprocals", (B * H, N))
    project(nc, x, wq, bq, wk, bk, wv, bv, ident, qs, ks, vs)
    attend(nc, mask_kq, mask_qk, tab_mul, ident, qs, ks, vs, ao)
    finish(nc, x, wo, bo, w_gate, w_up, w_down, ident, ao, rden, out)


def tables():
    key, query = np.arange(P)[:, None], np.arange(N)[None, :]
    mask = np.where(key > query[:, :P], MASKED, 0.0).astype(np.float32)
    decay = np.maximum(query - key, 1).astype(np.float64) ** -DECAY
    return mask, np.ascontiguousarray(mask.T), decay.astype(np.float32)


def kernel(**inputs):
    import concourse.bacc as bacc
    from concourse.bass_utils import run_bass_kernel_spmd

    nc = bacc.Bacc("TRN2", target_bir_lowering=False, num_devices=1)
    names = ["L0_attn_" + n for n in ("x", "Wq", "bq", "Wk", "bk", "Wv", "bv", "Wo", "bo")]
    names += ["L0_ffn_" + n for n in ("w_gate", "w_up", "w_down")]
    arrays = {n: np.ascontiguousarray(inputs[n]) for n in names}
    arrays |= dict(zip(("mask_keys_queries", "mask_queries_keys", "decay"), tables()))
    arrays["identity"] = np.eye(P, dtype=np.float32)
    args = [nc.dram_tensor(n, a.shape, mybir.dt.from_np(a.dtype), kind="ExternalInput").ap()
            for n, a in arrays.items()]
    out = nc.dram_tensor("out", (B, N, D), F32, kind="ExternalOutput").ap()
    build(nc, *args, out)
    return run_bass_kernel_spmd(nc, [arrays], core_ids=[0]).results[0]["out"]
```
